# Optimizing a Trainium2 kernel written in Bass

```python
import numpy as np
import jax
import jax.numpy as jnp

def _softmax(x, axis=-1):
    return jax.nn.softmax(x, axis=axis)

def _gelu(x):
    return jax.nn.gelu(x, approximate=True)

def _silu(x):
    return jax.nn.silu(x)

def _sigmoid(x):
    return jax.nn.sigmoid(x)

def _layernorm(x, axis=-1, eps=1e-05):
    m = jnp.mean(x, axis=axis, keepdims=True)
    v = jnp.var(x, axis=axis, keepdims=True)
    return (x - m) / jnp.sqrt(v + eps)

def _scatter_add(tgt, idx, src, axis=0):
    return tgt.at[idx].add(src)

def _segment_sum(src, seg, n):
    return jax.ops.segment_sum(src, seg, n)
kernel_name = 'mk_vit_tower_d1_tok_img768_r4_924ded'

def setup_inputs(seed: int=0):
    np.random.seed(seed)
    _w = jnp.asarray

    def _rec_inputs():
        import jax
        import jax.numpy as jnp
        _rk = jax.random.key(seed)
        x = -0.000348323 + 0.999952 * jax.random.normal(jax.random.fold_in(_rk, 1), (8, 3, 128, 128), jnp.float32)
        return x
    x = _rec_inputs()

    def _L0_tok_setup():
        import jax, jax.numpy as jnp
        import numpy as np
        PATCH = 16

        def _shifted_concat(x):
            B, C, H, W = x.shape
            xp = jnp.pad(x, ((0, 0), (0, 0), (1, 1), (1, 1)))
            right = xp[:, :, 1:1 + H, 0:W]
            left = xp[:, :, 1:1 + H, 2:2 + W]
            down = xp[:, :, 0:H, 1:1 + W]
            up = xp[:, :, 2:2 + H, 1:1 + W]
            return jnp.concatenate([x, right, left, down, up], axis=1)

        def _patchify(x, p):
            B, C, H, W = x.shape
            h, w = (H // p, W // p)
            x = x.reshape(B, C, h, p, w, p)
            x = x.transpose(0, 2, 4, 3, 5, 1)
            return x.reshape(B, h * w, p * p * C)

        def _layernorm(x, gamma, beta, eps=1e-05):
            mu = jnp.mean(x, axis=-1, keepdims=True)
            var = jnp.var(x, axis=-1, keepdims=True)
            return (x - mu) * jax.lax.rsqrt(var + eps) * gamma + beta
        key = jax.random.key(seed)
        k1, k2 = jax.random.split(key)
        B, H, W = (32, 96, 96)
        patch_dim = PATCH * PATCH * 15
        d_hidn = 192
        x = jax.random.normal(k1, (B, 3, H, W), dtype=jnp.float32)
        gamma = jnp.ones((patch_dim,), dtype=jnp.float32)
        beta = jnp.zeros((patch_dim,), dtype=jnp.float32)
        W_ = jax.random.normal(k2, (patch_dim, d_hidn), dtype=jnp.float32) * patch_dim ** (-0.5)
        b = jnp.zeros((d_hidn,), dtype=jnp.float32)
        return {'x': x, 'gamma': gamma, 'beta': beta, 'W': W_, 'b': b}
    _L0_tok_all = _L0_tok_setup()
    _L0_tok_in = {k: v for k, v in _L0_tok_all.items() if k in ('gamma', 'beta', 'W', 'b')}
    del _L0_tok_all

    def _L0_attn_setup():
        import jax, jax.numpy as jnp
        import numpy as np
        D_MODEL = 192
        D_STATE = 64
        D_CONV = 4
        EXPAND = 2
        HEADDIM = 64
        CHUNK = 64
        D_INNER = EXPAND * D_MODEL
        NHEADS = D_INNER // HEADDIM
        D_IN_PROJ = 2 * D_INNER + 2 * D_STATE + NHEADS
        CONV_DIM = D_INNER + 2 * D_STATE
        B_SZ = 8
        SEQ = 1024

        def _segsum(x):
            T = x.shape[-1]
            lower_strict = jnp.tril(jnp.ones((T, T), bool), -1)
            xe = jnp.where(lower_strict, x[..., :, None], 0.0)
            s = jnp.cumsum(xe, axis=-2)
            lower = jnp.tril(jnp.ones((T, T), bool), 0)
            return jnp.where(lower, s, -jnp.inf)

        def _ssd(x, A, B, C, chunk):
            b, L, h, p = x.shape
            c = L // chunk
            n = B.shape[-1]
            x = x.reshape(b, c, chunk, h, p)
            A = A.reshape(b, c, chunk, h).transpose(0, 3, 1, 2)
            B = B.reshape(b, c, chunk, 1, n)
            C = C.reshape(b, c, chunk, 1, n)
            A_cs = jnp.cumsum(A, axis=-1)
            Lmat = jnp.exp(_segsum(A))
            Y_diag = jnp.einsum('bclhn,bcshn,bhcls,bcshp->bclhp', C, B, Lmat, x)
            decay_states = jnp.exp(A_cs[..., -1:] - A_cs)
            states = jnp.einsum('bclhn,bhcl,bclhp->bchpn', B, decay_states, x)
            states = jnp.concatenate([jnp.zeros_like(states[:, :1]), states], axis=1)
            A_last = jnp.pad(A_cs[..., -1], ((0, 0), (0, 0), (1, 0)))
            decay_chunk = jnp.exp(_segsum(A_last))
            new_states = jnp.einsum('bhzc,bchpn->bzhpn', decay_chunk, states)
            states = new_states[:, :-1]
            Y_off = jnp.einsum('bclhn,bchpn,bhcl->bclhp', C, states, jnp.exp(A_cs))
            return (Y_diag + Y_off).reshape(b, L, h, p)
        key = jax.random.key(seed)
        ks = jax.random.split(key, 6)
        u = jax.random.normal(ks[0], (B_SZ, SEQ, D_MODEL), jnp.float32)
        W_in = jax.random.normal(ks[1], (D_IN_PROJ, D_MODEL), jnp.float32) / np.sqrt(D_MODEL).astype(np.float32)
        conv_w = jax.random.normal(ks[2], (CONV_DIM, 1, D_CONV), jnp.float32) / np.sqrt(D_CONV).astype(np.float32)
        conv_b = jnp.zeros((CONV_DIM,), jnp.float32)
        dt_bias = jax.random.uniform(ks[3], (NHEADS,), jnp.float32, -4.0, 1.0)
        A_log = jnp.full((NHEADS,), -np.log(2.0), jnp.float32)
        D_param = jnp.ones((NHEADS,), jnp.float32)
        norm_w = jnp.ones((D_INNER,), jnp.float32)
        W_out = jax.random.normal(ks[4], (D_MODEL, D_INNER), jnp.float32) / np.sqrt(D_INNER).astype(np.float32)
        return dict(u=u, W_in=W_in, conv_w=conv_w, conv_b=conv_b, dt_bias=dt_bias, A_log=A_log, D_param=D_param, norm_w=norm_w, W_out=W_out)
    _L0_attn_all = _L0_attn_setup()
    _L0_attn_in = {k: v for k, v in _L0_attn_all.items() if k in ('W_in', 'conv_w', 'conv_b', 'dt_bias', 'A_log', 'D_param', 'norm_w', 'W_out')}
    del _L0_attn_all

    def _L0_ffn_setup():
        import jax, jax.numpy as jnp
        import numpy as np
        D_MODEL = 192
        D_FF = 768
        N_EXPERTS = 9
        key = jax.random.key(seed)
        ks = jax.random.split(key, 7)
        scale = 0.02
        return {'x': jax.random.normal(ks[0], (2, 256, D_MODEL), jnp.float32), 'Ws': jax.random.normal(ks[1], (D_MODEL, N_EXPERTS), jnp.float32) * scale, 'bs': jnp.zeros((N_EXPERTS,), jnp.float32), 'W1': jax.random.normal(ks[2], (N_EXPERTS, D_MODEL, D_FF), jnp.float32) * scale, 'b1': jnp.zeros((N_EXPERTS, D_FF), jnp.float32), 'W2': jax.random.normal(ks[3], (N_EXPERTS, D_FF, D_MODEL), jnp.float32) * scale, 'b2': jnp.zeros((N_EXPERTS, D_MODEL), jnp.float32)}
    _L0_ffn_all = _L0_ffn_setup()
    _L0_ffn_in = {k: v for k, v in _L0_ffn_all.items() if k in ('Ws', 'bs', 'W1', 'b1', 'W2', 'b2')}
    del _L0_ffn_all
    return {'x': x, 'L0_tok_gamma': _L0_tok_in['gamma'], 'L0_tok_beta': _L0_tok_in['beta'], 'L0_tok_W': _L0_tok_in['W'], 'L0_tok_b': _L0_tok_in['b'], 'L0_attn_W_in': _L0_attn_in['W_in'], 'L0_attn_conv_w': _L0_attn_in['conv_w'], 'L0_attn_conv_b': _L0_attn_in['conv_b'], 'L0_attn_dt_bias': _L0_attn_in['dt_bias'], 'L0_attn_A_log': _L0_attn_in['A_log'], 'L0_attn_D_param': _L0_attn_in['D_param'], 'L0_attn_norm_w': _L0_attn_in['norm_w'], 'L0_attn_W_out': _L0_attn_in['W_out'], 'L0_ffn_Ws': _L0_ffn_in['Ws'], 'L0_ffn_bs': _L0_ffn_in['bs'], 'L0_ffn_W1': _L0_ffn_in['W1'], 'L0_ffn_b1': _L0_ffn_in['b1'], 'L0_ffn_W2': _L0_ffn_in['W2'], 'L0_ffn_b2': _L0_ffn_in['b2']}

def reference(x, L0_tok_gamma, L0_tok_beta, L0_tok_W, L0_tok_b, L0_attn_W_in, L0_attn_conv_w, L0_attn_conv_b, L0_attn_dt_bias, L0_attn_A_log, L0_attn_D_param, L0_attn_norm_w, L0_attn_W_out, L0_ffn_Ws, L0_ffn_bs, L0_ffn_W1, L0_ffn_b1, L0_ffn_W2, L0_ffn_b2):
    import jax
    import jax.numpy as jnp

    def _L0_tok_ref(x, gamma, beta, W, b):
        import jax, jax.numpy as jnp
        import numpy as np
        PATCH = 16

        def _shifted_concat(x):
            B, C, H, W = x.shape
            xp = jnp.pad(x, ((0, 0), (0, 0), (1, 1), (1, 1)))
            right = xp[:, :, 1:1 + H, 0:W]
            left = xp[:, :, 1:1 + H, 2:2 + W]
            down = xp[:, :, 0:H, 1:1 + W]
            up = xp[:, :, 2:2 + H, 1:1 + W]
            return jnp.concatenate([x, right, left, down, up], axis=1)

        def _patchify(x, p):
            B, C, H, W = x.shape
            h, w = (H // p, W // p)
            x = x.reshape(B, C, h, p, w, p)
            x = x.transpose(0, 2, 4, 3, 5, 1)
            return x.reshape(B, h * w, p * p * C)

        def _layernorm(x, gamma, beta, eps=1e-05):
            mu = jnp.mean(x, axis=-1, keepdims=True)
            var = jnp.var(x, axis=-1, keepdims=True)
            return (x - mu) * jax.lax.rsqrt(var + eps) * gamma + beta
        xs = _shifted_concat(x)
        tokens = _patchify(xs, PATCH)
        normed = _layernorm(tokens, gamma, beta)
        return jnp.einsum('bnd,de->bne', normed, W) + b

    def _L0_attn_ref(u, W_in, conv_w, conv_b, dt_bias, A_log, D_param, norm_w, W_out):
        import jax, jax.numpy as jnp
        import numpy as np
        D_MODEL = 192
        D_STATE = 64
        D_CONV = 4
        EXPAND = 2
        HEADDIM = 64
        CHUNK = 64
        D_INNER = EXPAND * D_MODEL
        NHEADS = D_INNER // HEADDIM
        D_IN_PROJ = 2 * D_INNER + 2 * D_STATE + NHEADS
        CONV_DIM = D_INNER + 2 * D_STATE
        B_SZ = 8
        SEQ = 1024

        def _segsum(x):
            T = x.shape[-1]
            lower_strict = jnp.tril(jnp.ones((T, T), bool), -1)
            xe = jnp.where(lower_strict, x[..., :, None], 0.0)
            s = jnp.cumsum(xe, axis=-2)
            lower = jnp.tril(jnp.ones((T, T), bool), 0)
            return jnp.where(lower, s, -jnp.inf)

        def _ssd(x, A, B, C, chunk):
            b, L, h, p = x.shape
            c = L // chunk
            n = B.shape[-1]
            x = x.reshape(b, c, chunk, h, p)
            A = A.reshape(b, c, chunk, h).transpose(0, 3, 1, 2)
            B = B.reshape(b, c, chunk, 1, n)
            C = C.reshape(b, c, chunk, 1, n)
            A_cs = jnp.cumsum(A, axis=-1)
            Lmat = jnp.exp(_segsum(A))
            Y_diag = jnp.einsum('bclhn,bcshn,bhcls,bcshp->bclhp', C, B, Lmat, x)
            decay_states = jnp.exp(A_cs[..., -1:] - A_cs)
            states = jnp.einsum('bclhn,bhcl,bclhp->bchpn', B, decay_states, x)
            states = jnp.concatenate([jnp.zeros_like(states[:, :1]), states], axis=1)
            A_last = jnp.pad(A_cs[..., -1], ((0, 0), (0, 0), (1, 0)))
            decay_chunk = jnp.exp(_segsum(A_last))
            new_states = jnp.einsum('bhzc,bchpn->bzhpn', decay_chunk, states)
            states = new_states[:, :-1]
            Y_off = jnp.einsum('bclhn,bchpn,bhcl->bclhp', C, states, jnp.exp(A_cs))
            return (Y_diag + Y_off).reshape(b, L, h, p)
        b, L, _ = u.shape
        zxbcdt = u @ W_in.T
        z = zxbcdt[..., :D_INNER]
        xBC = zxbcdt[..., D_INNER:D_INNER + CONV_DIM]
        dt = jax.nn.softplus(zxbcdt[..., D_INNER + CONV_DIM:] + dt_bias)
        xBC = jax.lax.conv_general_dilated(xBC.transpose(0, 2, 1), conv_w, window_strides=(1,), padding=[(D_CONV - 1, 0)], dimension_numbers=('NCH', 'OIH', 'NCH'), feature_group_count=CONV_DIM)
        xBC = jax.nn.silu(xBC.transpose(0, 2, 1) + conv_b)
        x = xBC[..., :D_INNER].reshape(b, L, NHEADS, HEADDIM)
        Bm = xBC[..., D_INNER:D_INNER + D_STATE][:, :, None, :]
        Cm = xBC[..., D_INNER + D_STATE:][:, :, None, :]
        A = -jnp.exp(A_log)
        Y = _ssd(x * dt[..., None], A * dt, Bm, Cm, CHUNK)
        y = Y + x * D_param[:, None]
        y = y.reshape(b, L, D_INNER)
        y = y * jax.nn.silu(z)
        y = y * jax.lax.rsqrt(jnp.mean(y * y, axis=-1, keepdims=True) + 1e-05) * norm_w
        return y @ W_out.T

    def _L0_ffn_ref(x, Ws, bs, W1, b1, W2, b2):
        import jax, jax.numpy as jnp
        import numpy as np
        D_MODEL = 192
        D_FF = 768
        N_EXPERTS = 9
        B, S, d = x.shape
        xt = x.reshape(-1, d)
        route_prob = jax.nn.softmax(xt @ Ws + bs, axis=-1)
        p = jnp.max(route_prob, axis=-1)
        routes = jnp.argmax(route_prob, axis=-1)
        h = jax.nn.gelu(jnp.einsum('td,edf->tef', xt, W1) + b1, approximate=False)
        out = jnp.einsum('tef,efd->ted', h, W2) + b2
        common = out[:, 0, :]
        sel = jnp.take_along_axis(out, routes[:, None, None], axis=1)[:, 0, :]
        scaling = (p / jax.lax.stop_gradient(p))[:, None]
        pe = p[:, None]
        final = jnp.where((routes == 0)[:, None], common * scaling, pe * sel + (1.0 - pe) * common)
        return final.reshape(B, S, d)
    h = _L0_tok_ref(x, L0_tok_gamma, L0_tok_beta, L0_tok_W, L0_tok_b)
    h = h + _L0_attn_ref(_layernorm(h, axis=-1), L0_attn_W_in, L0_attn_conv_w, L0_attn_conv_b, L0_attn_dt_bias, L0_attn_A_log, L0_attn_D_param, L0_attn_norm_w, L0_attn_W_out)
    h = h + _L0_ffn_ref(_layernorm(h, axis=-1), L0_ffn_Ws, L0_ffn_bs, L0_ffn_W1, L0_ffn_b1, L0_ffn_W2, L0_ffn_b2)
    return h

_drawn_inputs = setup_inputs


def setup_inputs(seed=0):
    import zlib

    import numpy as np

    out = dict(_drawn_inputs(seed))
    spreads = {'L0_tok_gamma': (1.0, 0.2),
     'L0_tok_beta': (0.0, 0.1),
     'L0_tok_b': (0.0, 0.1),
     'L0_attn_conv_b': (0.0, 0.1),
     'L0_attn_A_log': (-0.6931471824645996, 0.2),
     'L0_attn_D_param': (1.0, 0.2),
     'L0_attn_norm_w': (1.0, 0.2),
     'L0_ffn_bs': (0.0, 0.8),
     'L0_ffn_b1': (0.0, 0.471),
     'L0_ffn_b2': (0.0, 0.1)}
    factors = {'L0_ffn_Ws': 4.034}
    for name, (base, spread) in spreads.items():
        noise = np.random.default_rng([zlib.crc32(name.encode()), seed]).standard_normal(out[name].shape)
        drawn = base * np.exp(spread * noise) if base else spread * noise
        out[name] = jnp.asarray(drawn.astype(out[name].dtype))
    for name, factor in factors.items():
        out[name] = (out[name] * factor).astype(out[name].dtype)
    return out
```

```python
import concourse.bass as bass
from concourse import mybir
from contextlib import ExitStack

FP32 = mybir.dt.float32
I32 = mybir.dt.int32
ALU = mybir.AluOpType
ACT = mybir.ActivationFunctionType
AX = mybir.AxisListType

P = 128
TOKENS, D = 512, 192
TILES = TOKENS // P
IMGS, SEQ = 8, 64
PATCH, CH = 16, 3
SHIFTS = 5
FEATS = PATCH * PATCH * CH * SHIFTS
EXT = PATCH + 2
KT = 8
DH = D // 2
DI, DS, NH, HD = 384, 64, 6, 64
NC4 = (DI + 2 * DS) // P
TAPS = 4
XB = (0, 1, 2, 0)
YB = (3, 1, 2, 0)
NE, FF = 9, 768
FC = FF // P
EPS = 1e-5
MAGIC = 0x5F3759DF

C_ID, C_STRICT, C_CUM = 0, P, 2 * P
C_MULT = 3 * P
C_IOTA = C_MULT + KT
C_N = C_IOTA + NE
V_GAMMA, V_BETA = 0, SHIFTS * KT
V_TOKB = 2 * SHIFTS * KT
V_CW = V_TOKB + D
V_CB = V_CW + NC4 * TAPS
V_DTB = V_CB + NC4
V_ALOG = V_DTB + NH
V_DPAR = V_ALOG + NH
V_NW = V_DPAR + NH
V_BS = V_NW + DI // P
V_B1 = V_BS + NE
V_N = V_B1 + NE * FC


def vit_tower(nc, xT_d, wtok_d, const_d, vec_d, win_d, wout_d, ws_d, b2_d, w1_d, w2_d, out_d):
    ctx = ExitStack()
    with ctx:
        def sb(name, shape, dt=FP32):
            return ctx.enter_context(nc.sbuf_tensor(name, shape, dt))

        def sem(name):
            return ctx.enter_context(nc.semaphore(name))

        cst = sb("cst", [P, C_N])
        vec = sb("vec", [P, V_N])
        win = sb("win", [DH, 2, 2 * DI + 2 * DS + NH])
        wout = sb("wout", [P, DI // P, D])
        ws = sb("ws", [DH, 2, NE])
        b2 = sb("b2", [NE, D])
        w1 = sb("w1", [DH, NE, 2, FF])
        w2 = sb("w2", [P, NE, FC, D])
        ones = sb("ones", [P, P])
        arena = sb("arena", [P, 14352])
        place = [0]

        def view(*dims):
            n = 1
            for d in dims:
                n *= d
            a = arena[:, place[0]:place[0] + n]
            place[0] += n
            if len(dims) == 2:
                a = a.rearrange("p (a b) -> p a b", b=dims[1])
            if len(dims) == 3:
                a = a.rearrange("p (a b c) -> p a b c", b=dims[1], c=dims[2])
            return a

        wtok = view(KT, SHIFTS, D)
        xT = view(KT, TOKENS)
        wc = view(KT, D + 1)
        xT2 = view(2, TOKENS)
        place[0] = 0
        acc = view(NC4, TOKENS)
        xs = view(DI // P, TOKENS)
        Bt = view(TOKENS)
        Ct = view(TOKENS)
        zs = view(TILES, DI)
        segr = view(2, NH, P)
        E = view(2, NH, P)
        x_tm = view(TILES, DI)
        xdt = view(TILES, DI)
        xD = view(TILES, DI)
        GTm = view(TILES, P)
        place[0] = 0
        hT = view(FC, TOKENS)

        csc = sb("csc", [P, 2 * D])
        h = sb("h", [P, TILES, D])
        u = sb("u", [P, TILES, D])
        uT = sb("uT", [DH, 2, TOKENS])
        yzT = sb("yzT", [P, TILES, DI])
        coefT = sb("coefT", [NE, TOKENS])
        mv = sb("mv", [P, TILES, 2])
        bns = sb("bns", [P, TILES, 6])
        bna = sb("bna", [P, TILES, 2])
        var = sb("var", [P, TILES])
        rs_i = sb("rs_i", [P, TILES], I32)
        rs_y = sb("rs_y", [P, TILES])
        rs_t = sb("rs_t", [P, TILES])
        nmr = sb("nmr", [P, TILES])
        dtx = sb("dtx", [P, TILES, NH])
        dta = sb("dta", [P, TILES, NH])
        dt = sb("dt", [P, TILES, NH])
        adt = sb("adt", [P, TILES, NH])
        ea = sb("ea", [P, NH])
        ss = sb("ss", [P, TILES])
        sq = sb("sq", [P, DI])
        lg = sb("lg", [P, TILES, NE])
        ex = sb("ex", [P, TILES, NE])
        oh = sb("oh", [P, TILES, NE])
        coef = sb("coef", [P, TILES, NE])
        m4 = sb("m4", [P, TILES])
        p4 = sb("p4", [P, TILES])
        s4 = sb("s4", [P, TILES])
        ps = ctx.enter_context(nc.psum_tensor("ps", [P, 8, 512], FP32))

        ident = cst[:, C_ID:C_ID + P]
        strict = cst[:, C_STRICT:C_STRICT + P]
        cum = cst[:, C_CUM:C_CUM + P]
        iota = cst[:, C_IOTA:C_IOTA + NE]
        XC0 = DI + NH

        s_cst, s_vec, s_win, s_wout, s_small = (sem(n) for n in ("s_cst", "s_vec", "s_win", "s_wout", "s_small"))
        s_x = [sem(f"s_x{i}") for i in range(4)]
        s_wt = [sem(f"s_wt{t}") for t in range(KT)]
        s_w1 = [sem(f"s_w1_{e}") for e in range(NE)]
        s_w2 = [sem(f"s_w2_{e}") for e in range(NE)]
        s_ones, s_wc, s_mult, s_sq = sem("s_ones"), sem("s_wc"), sem("s_mult"), sem("s_sq")
        s_sqd, s_tok = sem("s_sqd"), sem("s_tok")
        s_u, s_ut, s_utc = sem("s_u"), sem("s_ut"), sem("s_utc")
        s_xbc, s_z, s_cv0, s_cv, s_xs = (sem(n) for n in ("s_xbc", "s_z", "s_cv0", "s_cv", "s_xs"))
        s_dtx, s_sp, s_ea, s_zs, s_adt = (sem(n) for n in ("s_dtx", "s_sp", "s_ea", "s_zs", "s_adt"))
        s_segr, s_seg, s_E, s_gt, s_gtm = (sem(n) for n in ("s_segr", "s_seg", "s_E", "s_gt", "s_gtm"))
        s_xt, s_xtm, s_xD, s_xdt, s_M = (sem(n) for n in ("s_xt", "s_xtm", "s_xD", "s_xdt", "s_M"))
        s_y, s_yz, s_ss, s_yt, s_ytc, s_o = (sem(n) for n in ("s_y", "s_yz", "s_ss", "s_yt", "s_ytc", "s_o"))
        s_wo, s_u2, s_u2t, s_u2c, s_lg = (sem(n) for n in ("s_wo", "s_u2", "s_u2t", "s_u2c", "s_lg"))
        s_lgs, s_ex, s_coef, s_ct, s_ctc = (sem(n) for n in ("s_lgs", "s_ex", "s_coef", "s_ct", "s_ctc"))
        s_b2o, s_hid, s_gel, s_eo, s_acc, s_out = (sem(n) for n in ("s_b2o", "s_hid", "s_gel", "s_eo", "s_acc", "s_out"))
        c_dve, c_act, c_pool = sem("c_dve"), sem("c_act"), sem("c_pool")

        block = ctx.enter_context(nc.Block())

        @block.sync
        def _(sp):
            sp.dma_start(vec[:], vec_d).then_inc(s_vec, 16)
            for t in range(KT):
                sp.dma_start(wtok[:, t], wtok_d[t]).then_inc(s_wt[t], 16)
            sp.dma_start(win[:], win_d).then_inc(s_win, 16)
            sp.dma_start(wout[:], wout_d).then_inc(s_wout, 16)
            sp.dma_start(ws[:], ws_d).then_inc(s_small, 16)
            sp.dma_start(b2[:], b2_d).then_inc(s_small, 16)
            for e in range(NE):
                sp.dma_start(w1[:, e], w1_d[e]).then_inc(s_w1[e], 16)
                sp.dma_start(w2[:, e], w2_d[e]).then_inc(s_w2[e], 16)
            for i in range(TILES):
                sp.wait_ge(s_acc, TILES * (NE + 1) - TILES + i + 1)
                sp.dma_start(out_d[i * P:(i + 1) * P, :], h[:, i]).then_inc(s_out, 16)
            sp.wait_ge(s_out, 16 * TILES)

        @block.gpsimd
        def _(pool):
            pool.memset(ones[:], 1.0).then_inc(s_ones, 1)
            pool.wait_ge(s_vec, 16)
            pool.wait_ge(s_wout, 16)
            for c in range(DI // P):
                pool.tensor_scalar(wout[:, c], wout[:, c], vec[:, V_NW + c:V_NW + c + 1], None,
                                   ALU.mult).then_inc(s_wo, 1)
            pool.wait_ge(s_cst, 16)
            for i in range(TILES):
                pool.wait_ge(s_adt, 1)
                if i >= 2:
                    pool.wait_ge(s_seg, i - 1)
                a = adt[:, i, :].unsqueeze(2).to_broadcast([P, NH, P])
                c = cum.unsqueeze(1).to_broadcast([P, NH, P])
                pool.tensor_tensor(segr[:, i % 2], c, a, ALU.mult).then_inc(s_segr, 1)
            for i in range(TILES):
                pool.wait_ge(s_xtm, i + 1)
                dpar = vec[:, V_DPAR:V_DPAR + NH].unsqueeze(2).to_broadcast([P, NH, HD])
                x3 = x_tm[:, i].rearrange("p (h d) -> p h d", d=HD)
                o3 = xD[:, i].rearrange("p (h d) -> p h d", d=HD)
                pool.tensor_tensor(o3, x3, dpar, ALU.mult).then_inc(s_xD, 1)

        @block.scalar
        def _(act):
            done = [0]

            def link(ins):
                done[0] += 1
                ins.then_inc(c_act, 1)
                act.wait_ge(c_act, done[0])

            act.dma_start(cst[:], const_d).then_inc(s_cst, 16)
            for g in range(KT // 2):
                act.dma_start(xT[:, 2 * g:2 * g + 2], xT_d[:, 2 * g:2 * g + 2]).then_inc(s_x[g], 16)
            for t in range(KT):
                act.wait_ge(s_x[t // 2], 16)
                if t >= 2:
                    act.wait_ge(s_sqd, t - 1)
                act.activation(xT2[:, t % 2], xT[:, t], ACT.Square).then_inc(s_sq, 1)
            act.wait_ge(s_vec, 16)
            act.activation(ea[:], vec[:, V_ALOG:V_ALOG + NH], ACT.Exp).then_inc(s_ea, 1)
            act.wait_ge(s_ut, 2)
            act.activation(uT[:, 0], ps[0:DH, 5], ACT.Copy).then_inc(s_utc, 1)
            for n in range(NC4):
                c = (n + 3) % NC4
                act.wait_ge(s_xbc, n + 1)
                act.activation(acc[:, c], ps[:, c], ACT.Identity,
                               bias=vec[:, V_CB + c:V_CB + c + 1],
                               scale=vec[:, V_CW + c * TAPS + TAPS - 1:V_CW + c * TAPS + TAPS]).then_inc(s_cv0, 1)
            act.wait_ge(s_dtx, 1)
            link(act.activation(dta[:], dtx[:], ACT.Abs))
            link(act.activation(dta[:], dta[:], ACT.Exp, scale=-1.0))
            act.activation(dta[:], dta[:], ACT.Ln, bias=1.0).then_inc(s_sp, 1)
            for i in range(TILES):
                act.activation(zs[:, i], ps[:, 4 + i, 0:DI], ACT.Silu).then_inc(s_zs, 1)
            for n in range(NC4):
                c = (n + 3) % NC4
                act.wait_ge(s_cv, n + 1)
                if c == 3:
                    act.activation(Bt[0:DS, :], acc[0:DS, c], ACT.Silu).then_inc(s_xs, 1)
                    act.activation(Ct[0:DS, :], acc[DS:P, c], ACT.Silu).then_inc(s_xs, 1)
                else:
                    act.activation(xs[:, c], acc[:, c], ACT.Silu).then_inc(s_xs, 1)

            def decay(i):
                act.wait_ge(s_seg, i + 1)
                if i >= 2:
                    act.wait_ge(s_y, i - 1)
                b = 4 + 2 * (i % 2)
                act.activation(E[:, i % 2].rearrange("p (g h) l -> p g (h l)", g=2), ps[:, b:b + 2, 0:DI],
                               ACT.Exp).then_inc(s_E, 1)

            decay(0)
            decay(1)
            for i in range(TILES):
                act.wait_ge(s_xt, i + 1)
                act.activation(x_tm[:, i], ps[:, XB[i], 0:DI], ACT.Copy).then_inc(s_xtm, 1)
            decay(2)
            decay(3)
            for i in range(TILES):
                act.wait_ge(s_yz, i + 1)
                if i:
                    act.wait_ge(s_ss, i)
                act.activation(sq[:], x_tm[:, i], ACT.Square, accum_out=ss[:, i:i + 1]).then_inc(s_ss, 1)
                act.wait_ge(s_yt, i + 1)
                act.activation(yzT[:, i], ps[:, 4 + i, 0:DI], ACT.Copy).then_inc(s_ytc, 1)
            act.wait_ge(s_u2t, 2)
            act.activation(uT[:, 0], ps[0:DH, 4], ACT.Copy).then_inc(s_u2c, 1)
            act.wait_ge(s_lgs, 1)
            act.activation(ex[:], lg[:], ACT.Exp).then_inc(s_ex, 1)
            act.wait_ge(s_ct, 1)
            act.activation(coefT[:], ps[0:NE, 7], ACT.Copy).then_inc(s_ctc, 1)
            for e in range(NE):
                for f in range(FC):
                    n = e * FC + f
                    act.wait_ge(s_hid, n + 1)
                    if e >= 1 and f == 0:
                        act.wait_ge(s_eo, TILES * e)
                    act.activation(hT[:, f], ps[:, n % 2], ACT.Gelu,
                                   bias=vec[:, V_B1 + n:V_B1 + n + 1]).then_inc(s_gel, 1)

        @block.vector
        def _(dve):
            done = [0]

            def link(ins):
                done[0] += 1
                ins.then_inc(c_dve, 1)
                dve.wait_ge(c_dve, done[0])

            def rsqrt(v, y):
                link(dve.tensor_scalar(rs_i[:], v.bitcast(I32), 1, None, ALU.logical_shift_right))
                link(dve.tensor_scalar(y.bitcast(I32), rs_i[:], -1.0, float(MAGIC), ALU.mult, ALU.add))
                for _ in range(3):
                    link(dve.tensor_tensor(rs_t[:], y, y, ALU.mult))
                    link(dve.tensor_tensor(rs_t[:], rs_t[:], v, ALU.mult))
                    link(dve.tensor_scalar(rs_t[:], rs_t[:], -0.5, 1.5, ALU.mult, ALU.add))
                    link(dve.tensor_tensor(y, y, rs_t[:], ALU.mult))

            def layernorm():
                for i in range(TILES):
                    link(dve.bn_stats(bns[:, i], h[:, i]))
                for i in range(TILES):
                    link(dve.bn_aggr(bna[:, i], bns[:, i]))
                link(dve.tensor_scalar(var[:], bna[:, :, 1], EPS, None, ALU.add))
                rsqrt(var[:], rs_y[:])
                link(dve.scalar_tensor_tensor(nmr[:], bna[:, :, 0], -1.0, rs_y[:], ALU.mult, ALU.mult))

            dve.wait_ge(s_cst, 16)
            dve.tensor_copy(wc[:, :, D], cst[:, C_MULT:C_MULT + KT]).then_inc(s_mult, 1)
            dve.wait_ge(s_vec, 16)
            for t in range(KT):
                dve.wait_ge(s_wt[t], 16)
                for s in range(SHIFTS):
                    g = vec[:, V_GAMMA + s * KT + t:V_GAMMA + s * KT + t + 1]
                    if s == 0:
                        link(dve.tensor_scalar(wc[:, t, 0:D], wtok[:, t, s], g, None, ALU.mult))
                    elif s < SHIFTS - 1:
                        link(dve.scalar_tensor_tensor(wc[:, t, 0:D], wtok[:, t, s], g, wc[:, t, 0:D], ALU.mult, ALU.add))
                    else:
                        dve.scalar_tensor_tensor(wc[:, t, 0:D], wtok[:, t, s], g, wc[:, t, 0:D],
                                                 ALU.mult, ALU.add).then_inc(s_wc, 1)
            dve.wait_ge(s_tok, 1)
            link(dve.tensor_copy(csc[:, 0:D], ps[:, 4, 0:D]))
            link(dve.tensor_tensor(csc[:, D:2 * D], ps[:, 4, D:2 * D], vec[:, V_TOKB:V_TOKB + D], ALU.add))
            link(dve.tensor_scalar(mv[:], ps[:, 0:TILES, D:D + 2], 1.0 / FEATS, None, ALU.mult))
            link(dve.tensor_tensor(var[:], mv[:, :, 0], mv[:, :, 0], ALU.mult))
            link(dve.tensor_tensor(var[:], mv[:, :, 1], var[:], ALU.subtract))
            link(dve.tensor_scalar(var[:], var[:], 0.0, EPS, ALU.max, ALU.add))
            rsqrt(var[:], rs_y[:])
            link(dve.scalar_tensor_tensor(nmr[:], mv[:, :, 0], -1.0, rs_y[:], ALU.mult, ALU.mult))
            for i in range(TILES):
                link(dve.scalar_tensor_tensor(h[:, i], csc[:, 0:D], nmr[:, i:i + 1], csc[:, D:2 * D], ALU.mult, ALU.add))
                link(dve.scalar_tensor_tensor(h[:, i], ps[:, i, 0:D], rs_y[:, i:i + 1], h[:, i], ALU.mult, ALU.add))
            layernorm()
            for i in range(TILES):
                dve.tensor_scalar(u[:, i], h[:, i], rs_y[:, i:i + 1], nmr[:, i:i + 1],
                                  ALU.mult, ALU.add).then_inc(s_u, 1)
            dve.wait_ge(s_ut, 2)
            dve.tensor_copy(uT[:, 1], ps[0:DH, 6]).then_inc(s_utc, 1)
            dve.wait_ge(s_z, TILES)
            dtb = vec[:, V_DTB:V_DTB + NH].unsqueeze(1).to_broadcast([P, TILES, NH])
            dve.tensor_tensor(dtx[:], ps[:, 4:8, DI:DI + NH], dtb, ALU.add).then_inc(s_dtx, 1)
            dve.wait_ge(s_sp, 1)
            dve.wait_ge(s_ea, 1)
            link(dve.scalar_tensor_tensor(dt[:], dtx[:], 0.0, dta[:], ALU.max, ALU.add))
            eab = ea[:].unsqueeze(1).to_broadcast([P, TILES, NH])
            dve.scalar_tensor_tensor(adt[:], dt[:], -1.0, eab, ALU.mult, ALU.mult).then_inc(s_adt, 1)
            for n in range(NC4):
                c = (n + 3) % NC4
                dve.wait_ge(s_cv0, n + 1)
                for k in range(1, TAPS):
                    w = vec[:, V_CW + c * TAPS + TAPS - 1 - k:V_CW + c * TAPS + TAPS - k]
                    a3 = acc[:, c].rearrange("p (b l) -> p b l", l=SEQ)[:, :, k:]
                    p3 = ps[:, c].rearrange("p (b l) -> p b l", l=SEQ)[:, :, 0:SEQ - k]
                    ins = dve.scalar_tensor_tensor(a3, p3, w, a3, ALU.mult, ALU.add)
                    if k < TAPS - 1:
                        link(ins)
                    else:
                        ins.then_inc(s_cv, 1)
            dve.wait_ge(s_gt, 1)
            cumb = cum.unsqueeze(1).to_broadcast([P, TILES, P])
            link(dve.tensor_tensor(GTm[:], ps[:, 3].rearrange("p (t l) -> p t l", l=P), cumb, ALU.mult))

            def mix(i):
                dve.wait_ge(s_E, i + 1)
                g = GTm[:, i].unsqueeze(1).to_broadcast([P, NH, P])
                dve.tensor_tensor(E[:, i % 2], E[:, i % 2], g, ALU.mult).then_inc(s_M, 1)
                dve.wait_ge(s_xtm, i + 1)
                x3 = x_tm[:, i].rearrange("p (h d) -> p h d", d=HD)
                o3 = xdt[:, i].rearrange("p (h d) -> p h d", d=HD)
                dve.tensor_tensor(o3, x3, dt[:, i].unsqueeze(2).to_broadcast([P, NH, HD]), ALU.mult).then_inc(s_xdt, 1)

            def gate(i):
                dve.wait_ge(s_y, i + 1)
                dve.wait_ge(s_xD, i + 1)
                link(dve.tensor_tensor(xD[:, i], ps[:, YB[i], 0:DI], xD[:, i], ALU.add))
                dve.wait_ge(s_zs, TILES)
                dve.tensor_tensor(x_tm[:, i], xD[:, i], zs[:, i], ALU.mult).then_inc(s_yz, 1)

            mix(0)
            mix(1)
            gate(0)
            mix(2)
            gate(1)
            mix(3)
            gate(2)
            gate(3)
            dve.wait_ge(s_ss, TILES)
            link(dve.tensor_scalar(var[:], ss[:], 1.0 / DI, EPS, ALU.mult, ALU.add))
            rsqrt(var[:], rs_y[:])
            for i in range(TILES):
                dve.wait_ge(s_o, i + 1)
                link(dve.scalar_tensor_tensor(h[:, i], ps[:, YB[i], 0:D], rs_y[:, i:i + 1], h[:, i], ALU.mult, ALU.add))
            layernorm()
            for i in range(TILES):
                dve.tensor_scalar(u[:, i], h[:, i], rs_y[:, i:i + 1], nmr[:, i:i + 1],
                                  ALU.mult, ALU.add).then_inc(s_u2, 1)
            dve.wait_ge(s_u2t, 2)
            dve.tensor_copy(uT[:, 1], ps[0:DH, 5]).then_inc(s_u2c, 1)
            dve.wait_ge(s_lg, 1)
            bsb = vec[:, V_BS:V_BS + NE].unsqueeze(1).to_broadcast([P, TILES, NE])
            iob = iota.unsqueeze(1).to_broadcast([P, TILES, NE])

            def wide(a):
                return a.unsqueeze(2).to_broadcast([P, TILES, NE])

            link(dve.tensor_tensor(lg[:], ps[:, 6, 0:TILES * NE].rearrange("p (t e) -> p t e", e=NE), bsb, ALU.add))
            link(dve.tensor_reduce(m4[:], lg[:], AX.X, ALU.max))
            dve.tensor_tensor(lg[:], lg[:], wide(m4[:]), ALU.subtract).then_inc(s_lgs, 1)
            dve.wait_ge(s_lgs, 1)
            link(dve.tensor_scalar(oh[:], lg[:], 0.0, -float(NE), ALU.is_equal, ALU.mult))
            link(dve.tensor_tensor(oh[:], oh[:], iob, ALU.add))
            link(dve.tensor_reduce(m4[:], oh[:], AX.X, ALU.min))
            link(dve.tensor_scalar(m4[:], m4[:], float(NE), None, ALU.add))
            link(dve.tensor_tensor(oh[:], iob, wide(m4[:]), ALU.is_equal))
            dve.wait_ge(s_ex, 1)
            link(dve.tensor_reduce(s4[:], ex[:], AX.X, ALU.add))
            link(dve.reciprocal(p4[:], s4[:]))
            link(dve.tensor_tensor(coef[:], oh[:], wide(p4[:]), ALU.mult))
            link(dve.tensor_scalar(s4[:], p4[:], -1.0, 1.0, ALU.mult, ALU.add))
            dve.tensor_tensor(coef[:, :, 0], coef[:, :, 0], s4[:], ALU.add).then_inc(s_coef, 1)
            for i in range(TILES):
                dve.wait_ge(s_b2o, i + 1)
                dve.tensor_tensor(h[:, i], h[:, i], ps[:, 2 + i % 2, 0:D], ALU.add).then_inc(s_acc, 1)
            for e in range(NE):
                for i in range(TILES):
                    dve.wait_ge(s_eo, TILES * e + i + 1)
                    dve.wait_ge(s_acc, TILES * e + i + 1)
                    dve.scalar_tensor_tensor(h[:, i], ps[:, 2 + i, 0:D], coef[:, i, e:e + 1], h[:, i],
                                             ALU.mult, ALU.add).then_inc(s_acc, 1)

        @block.tensor
        def _(pe):
            mm = pe.matmul
            pe.wait_ge(s_ones, 1)
            pe.wait_ge(s_vec, 16)
            pe.wait_ge(s_mult, 1)
            for t in range(KT):
                pe.wait_ge(s_wt[t], 16)
                for s in range(SHIFTS):
                    b = vec[:, V_BETA + s * KT + t:V_BETA + s * KT + t + 1].to_broadcast([P, P])
                    mm(ps[:, 4, D:2 * D], b, wtok[:, t, s], start=(t == 0 and s == 0),
                       stop=(t == KT - 1 and s == SHIFTS - 1), skip_group_check=True)
                pe.wait_ge(s_wc, t + 1)
                mm(ps[:, 4, 0:D], ones[:], wc[:, t, 0:D], start=False, stop=(t == KT - 1), skip_group_check=True)
                pe.wait_ge(s_x[t // 2], 16)
                for i in range(TILES):
                    mm(ps[:, i, 0:D + 1], xT[:, t, i * P:(i + 1) * P], wc[:, t], start=(t == 0),
                       stop=(t == KT - 1), skip_group_check=True)
                pe.wait_ge(s_sq, t + 1)
                for i in range(TILES):
                    last = mm(ps[:, i, D + 1:D + 2], xT2[:, t % 2, i * P:(i + 1) * P], wc[:, t, D:D + 1],
                              start=False, stop=(t == KT - 1), skip_group_check=True)
                last.then_inc(s_sqd, 1)
                if t == KT - 1:
                    mm(ps[:, 7, 0:1], ones[:, :], ones[:, 0:1], start=True, stop=True).then_inc(s_tok, 1)

            def turn(src, produced, banks, turned):
                for i in range(TILES):
                    pe.wait_ge(produced, i + 1)
                    for k in range(2):
                        last = pe.transpose(ps[0:DH, banks[k], i * P:(i + 1) * P],
                                            src[:, i, k * DH:(k + 1) * DH], ident)
                last.then_inc(turned, 2)

            pe.wait_ge(s_cst, 16)
            turn(u, s_u, (5, 6), s_ut)
            pe.wait_ge(s_utc, 2)
            pe.wait_ge(s_win, 16)
            for n in range(NC4):
                c = (n + 3) % NC4
                for k in range(2):
                    last = mm(ps[:, c], win[:, k, XC0 + c * P:XC0 + (c + 1) * P], uT[:, k],
                              start=(k == 0), stop=(k == 1))
                last.then_inc(s_xbc, 1)
            for i in range(TILES):
                for k in range(2):
                    last = mm(ps[:, 4 + i, 0:XC0], uT[:, k, i * P:(i + 1) * P], win[:, k, 0:XC0],
                              start=(k == 0), stop=(k == 1))
                last.then_inc(s_z, 1)

            def segments(i):
                pe.wait_ge(s_segr, i + 1)
                pe.wait_ge(s_zs, TILES)
                if i >= 2:
                    pe.wait_ge(s_E, i - 1)
                for g in range(2):
                    last = mm(ps[:, 4 + 2 * (i % 2) + g, 0:DI], strict,
                              segr[:, i % 2, 3 * g:3 * g + 3].rearrange("p h l -> p (h l)"), start=True, stop=True)
                last.then_inc(s_seg, 1)

            def ssd(i):
                pe.wait_ge(s_M, i + 1)
                pe.wait_ge(s_xdt, i + 1)
                pe.wait_ge(s_xtm, TILES)
                for n in range(NH):
                    last = mm(ps[:, YB[i], n * HD:(n + 1) * HD], E[:, i % 2, n], xdt[:, i, n * HD:(n + 1) * HD],
                              start=True, stop=True)
                last.then_inc(s_y, 1)

            def turn_y(i):
                pe.wait_ge(s_yz, i + 1)
                pe.wait_ge(s_E, 3 if i < 2 else 4)
                for c in range(DI // P):
                    last = pe.transpose(ps[:, 4 + i, c * P:(c + 1) * P], x_tm[:, i, c * P:(c + 1) * P], ident)
                last.then_inc(s_yt, 1)

            pe.wait_ge(s_xs, 2)
            for i in range(TILES):
                r = slice(i * P, (i + 1) * P)
                last = mm(ps[:, 3, r], Bt[0:DS, r], Ct[0:DS, r], start=True, stop=True)
            last.then_inc(s_gt, 1)
            segments(0)
            segments(1)
            pe.wait_ge(s_xs, NC4 + 1)
            for i in range(TILES):
                if i == 3:
                    pe.wait_ge(s_xtm, 1)
                for c in range(DI // P):
                    last = pe.transpose(ps[:, XB[i], c * P:(c + 1) * P], xs[:, c, i * P:(i + 1) * P], ident)
                last.then_inc(s_xt, 1)
            ssd(0)
            segments(2)
            ssd(1)
            segments(3)
            turn_y(0)
            ssd(2)
            turn_y(1)
            ssd(3)
            turn_y(2)
            turn_y(3)
            pe.wait_ge(s_wo, DI // P)
            for i in range(TILES):
                pe.wait_ge(s_ytc, i + 1)
                for c in range(DI // P):
                    last = mm(ps[:, YB[i], 0:D], yzT[:, i, c * P:(c + 1) * P], wout[:, c],
                              start=(c == 0), stop=(c == DI // P - 1))
                last.then_inc(s_o, 1)
            turn(u, s_u2, (4, 5), s_u2t)
            pe.wait_ge(s_u2c, 2)
            pe.wait_ge(s_small, 32)
            for i in range(TILES):
                for k in range(2):
                    last = mm(ps[:, 6, i * NE:(i + 1) * NE], uT[:, k, i * P:(i + 1) * P], ws[:, k],
                              start=(k == 0), stop=(k == 1))
            last.then_inc(s_lg, 1)
            pe.wait_ge(s_coef, 1)
            for i in range(TILES):
                last = pe.transpose(ps[0:NE, 7, i * P:(i + 1) * P], coef[:, i], ident)
            last.then_inc(s_ct, 1)
            pe.wait_ge(s_ctc, 1)
            for i in range(TILES):
                if i >= 2:
                    pe.wait_ge(s_acc, i - 1)
                mm(ps[:, 2 + i % 2, 0:D], coefT[:, i * P:(i + 1) * P], b2[:], start=True, stop=True).then_inc(s_b2o, 1)
            for e in range(NE):
                pe.wait_ge(s_w1[e], 16)
                for f in range(FC):
                    n = e * FC + f
                    if n >= 2:
                        pe.wait_ge(s_gel, n - 1)
                    for k in range(2):
                        last = mm(ps[:, n % 2], w1[:, e, k, f * P:(f + 1) * P], uT[:, k],
                                  start=(k == 0), stop=(k == 1))
                    last.then_inc(s_hid, 1)
                pe.wait_ge(s_w2[e], 16)
                for i in range(TILES):
                    pe.wait_ge(s_acc, TILES * e + i + 1 if e else TILES)
                    for f in range(FC):
                        if i == 0:
                            pe.wait_ge(s_gel, e * FC + f + 1)
                        last = mm(ps[:, 2 + i, 0:D], hT[:, f, i * P:(i + 1) * P], w2[:, e, f],
                                  start=(f == 0), stop=(f == FC - 1))
                    last.then_inc(s_eo, 1)


def kernel(**inputs):
    import numpy as np
    import concourse.bacc as bacc
    from concourse.bass_utils import run_bass_kernel_spmd

    a = {k: np.asarray(v) for k, v in inputs.items()}

    def wrap(rows):
        full = np.zeros((KT * P,) + rows.shape[1:], rows.dtype)
        full[:rows.shape[0]] = rows
        return np.moveaxis(full.reshape((KT, P) + rows.shape[1:]), 1, 0)

    xp = np.pad(a["x"], ((0, 0), (0, 0), (1, 1), (1, 1)))
    n = a["x"].shape[2] // PATCH
    cut = np.stack([xp[:, :, PATCH * i:PATCH * i + EXT, PATCH * j:PATCH * j + EXT]
                    for i in range(n) for j in range(n)], 1)
    xT = wrap(cut.transpose(3, 2, 4, 0, 1).reshape(EXT * CH * EXT, TOKENS))

    offset = [(1, 1), (1, 0), (1, 2), (0, 1), (2, 1)]

    def spread(v):
        v = v.reshape((PATCH, PATCH, SHIFTS, CH) + v.shape[1:])
        out = np.zeros((SHIFTS, EXT, CH, EXT) + v.shape[4:], v.dtype)
        for s, (r, c) in enumerate(offset):
            out[s, r:r + PATCH, :, c:c + PATCH] = np.swapaxes(v[:, :, s], 1, 2)
        out = np.moveaxis(out, 0, 3)
        return wrap(out.reshape((EXT * CH * EXT, SHIFTS) + v.shape[4:]))

    wtok = np.ascontiguousarray(spread(a["L0_tok_W"]).swapaxes(0, 1))
    gamma = spread(a["L0_tok_gamma"]).transpose(0, 2, 1).reshape(P, SHIFTS * KT)
    beta = spread(a["L0_tok_beta"]).transpose(0, 2, 1).reshape(P, SHIFTS * KT)

    def rows(v):
        return np.broadcast_to(v.reshape(1, -1), (P, v.size))

    def cols(v):
        v = v.reshape(-1, P, v.size // v.shape[0])
        return v.transpose(1, 0, 2).reshape(P, -1)

    vec = np.concatenate([gamma, beta, rows(a["L0_tok_b"]),
                          cols(a["L0_attn_conv_w"].reshape(-1, TAPS)), cols(a["L0_attn_conv_b"]),
                          rows(a["L0_attn_dt_bias"]), rows(a["L0_attn_A_log"]), rows(a["L0_attn_D_param"]),
                          cols(a["L0_attn_norm_w"]), rows(a["L0_ffn_bs"]), cols(a["L0_ffn_b1"].reshape(-1))], 1)
    w_in = a["L0_attn_W_in"].T
    z_end, xbc_end = DI, DI + DI + 2 * DS
    win = np.concatenate([w_in[:, :z_end], w_in[:, xbc_end:], w_in[:, z_end:xbc_end]], 1)
    win = win.reshape(2, DH, -1).transpose(1, 0, 2)
    wout = a["L0_attn_W_out"].T.reshape(DI // P, P, D).transpose(1, 0, 2)
    ws = a["L0_ffn_Ws"].reshape(2, DH, NE).transpose(1, 0, 2)
    w1 = a["L0_ffn_W1"].reshape(NE, 2, DH, FF).transpose(0, 2, 1, 3)
    w2 = a["L0_ffn_W2"].reshape(NE, FC, P, D).transpose(0, 2, 1, 3)

    k, m = np.arange(P)[:, None], np.arange(P)[None, :]
    same = k // SEQ == m // SEQ
    seen = np.zeros((EXT, CH, EXT), np.float32)
    for r, c in offset:
        seen[r:r + PATCH, :, c:c + PATCH] += 1
    const = np.concatenate([k == m, same & (k > m), same & (k <= m), wrap(seen.reshape(-1)),
                            np.broadcast_to(np.arange(NE), (P, NE))], 1).astype(np.float32)

    data = dict(xT=xT, wtok=wtok, const=const, vec=vec, win=win, wout=wout, ws=ws, b2=a["L0_ffn_b2"], w1=w1, w2=w2)
    nc = bacc.Bacc("TRN2", target_bir_lowering=False, num_devices=1)
    arrays, args = {}, []
    for name, v in data.items():
        arrays[name + "_dram"] = np.ascontiguousarray(v)
        args.append(nc.dram_tensor(name + "_dram", v.shape, mybir.dt.from_np(v.dtype), kind="ExternalInput").ap())
    args.append(nc.dram_tensor("out", (TOKENS, D), FP32, kind="ExternalOutput").ap())
    vit_tower(nc, *args)
    r = run_bass_kernel_spmd(nc, [arrays], core_ids=[0])
    return r.results[0]["out"].reshape(IMGS, SEQ, D)
```

```python
import concourse.bass as bass
from concourse import mybir
from contextlib import ExitStack

FP32 = mybir.dt.float32
I32 = mybir.dt.int32
U32 = mybir.dt.uint32
ALU = mybir.AluOpType
ACT = mybir.ActivationFunctionType
AX = mybir.AxisListType

P = 128
TOKENS, D = 512, 192
TILES = TOKENS // P
IMGS, SEQ = 8, 64
PATCH, CH = 16, 3
SHIFTS = 5
FEATS = PATCH * PATCH * CH * SHIFTS
EXT = PATCH + 2
KT = 8
DH = D // 2
DI, DS, NH, HD = 384, 64, 6, 64
NC4 = (DI + 2 * DS) // P
TAPS = 4
XB = (0, 1, 2, 0)
YB = (3, 1, 2, 0)
NE, FF = 9, 768
NR = NE - 1
FH = FF // 2
SLOTS = (TOKENS + NR * (P - 1)) // P
FC = FF // P
EPS = 1e-5
MAGIC = 0x5F3759DF

C_ID, C_STRICT, C_CUM = 0, P, 2 * P
C_MULT = 3 * P
C_IOTA = C_MULT + KT
C_BEFORE = C_IOTA + 16
C_LANE = C_BEFORE + P
C_TOK = C_LANE + P
C_N = C_TOK + TILES
V_GAMMA, V_BETA = 0, SHIFTS * KT
V_TOKB = 2 * SHIFTS * KT
V_CW = V_TOKB + D
V_CB = V_CW + NC4 * TAPS
V_DTB = V_CB + NC4
V_ALOG = V_DTB + NH
V_DPAR = V_ALOG + NH
V_NW = V_DPAR + NH
V_BS = V_NW + DI // P
V_B1 = V_BS + NE
V_N = V_B1 + FC


def vit_tower(nc, xT_d, wtok_d, const_d, vec_d, win_d, wout_d, ws_d, b2_d, b1_d, w1_d, w2_d, rows_d, sorted_d, out_d):
    ctx = ExitStack()
    with ctx:
        def sb(name, shape, dt=FP32):
            return ctx.enter_context(nc.sbuf_tensor(name, shape, dt))

        def sem(name):
            return ctx.enter_context(nc.semaphore(name))

        cst = sb("cst", [P, C_N])
        vec = sb("vec", [P, V_N])
        win = sb("win", [DH, 2, 2 * DI + 2 * DS + NH])
        wout = sb("wout", [P, DI // P, D])
        ws = sb("ws", [DH, 2, NE])
        b2 = sb("b2", [NE, D])
        w1 = sb("w1", [DH + 1, NE, 2, FF])
        w2 = sb("w2", [P, NE, FC, D])
        ones = sb("ones", [P, P])
        arena = sb("arena", [P, 14352])
        place = [0]

        def view(*dims):
            n = 1
            for d in dims:
                n *= d
            a = arena[:, place[0]:place[0] + n]
            place[0] += n
            if len(dims) == 2:
                a = a.rearrange("p (a b) -> p a b", b=dims[1])
            if len(dims) == 3:
                a = a.rearrange("p (a b c) -> p a b c", b=dims[1], c=dims[2])
            return a

        wtok = view(KT, SHIFTS, D)
        xT = view(KT, TOKENS)
        wc = view(KT, D + 1)
        xT2 = view(2, TOKENS)
        place[0] = 0
        acc = view(NC4, TOKENS)
        xs = view(DI // P, TOKENS)
        Bt = view(TOKENS)
        Ct = view(TOKENS)
        zs = view(TILES, DI)
        segr = view(2, NH, P)
        E = view(2, NH, P)
        x_tm = view(TILES, DI)
        xdt = view(TILES, DI)
        xD = view(TILES, DI)
        GTm = view(TILES, P)
        place[0] = 0
        hT = view(FC, TOKENS)
        xg = view(2, D)
        xgT = view(2, 2, P)
        hid = view(2, FF)
        hidT = view(2, FF)
        y_s = view(2, D)
        y_t = view(TILES, D)
        pos1 = view(TILES, P)

        csc = sb("csc", [P, 2 * D])
        h = sb("h", [P, TILES, D])
        u = sb("u", [P, TILES, D])
        uT = sb("uT", [DH, 2, TOKENS])
        yzT = sb("yzT", [P, TILES, DI])
        coefT = sb("coefT", [NE, TOKENS])
        mv = sb("mv", [P, TILES, 2])
        bns = sb("bns", [P, TILES, 6])
        bna = sb("bna", [P, TILES, 2])
        var = sb("var", [P, TILES])
        rs_i = sb("rs_i", [P, TILES], I32)
        rs_y = sb("rs_y", [P, TILES])
        rs_t = sb("rs_t", [P, TILES])
        nmr = sb("nmr", [P, TILES])
        dtx = sb("dtx", [P, TILES, NH])
        dta = sb("dta", [P, TILES, NH])
        dt = sb("dt", [P, TILES, NH])
        adt = sb("adt", [P, TILES, NH])
        ea = sb("ea", [P, NH])
        ss = sb("ss", [P, TILES])
        sq = sb("sq", [P, DI])
        lg = sb("lg", [P, TILES, NE])
        ex = sb("ex", [P, TILES, NE])
        oh = sb("oh", [P, TILES, NE])
        coef = sb("coef", [P, TILES, NE])
        m4 = sb("m4", [P, TILES])
        p4 = sb("p4", [P, TILES])
        gate_sel = sb("gate_sel", [P, TILES])
        cnt = sb("cnt", [P, 2, TILES, NR])
        tot = sb("tot", [P, NR])
        more = sb("more", [P, NR, TILES])
        need = sb("need", [P, NR])
        end = sb("end", [P, NR])
        base = sb("base", [P, TILES, NR])
        slot = sb("slot", [P, TILES])
        slot_u = sb("slot_u", [P, TILES], U32)
        s_hi = sb("s_hi", [P, TILES], I32)
        s_lo = sb("s_lo", [P, TILES], I32)
        f_hi = sb("f_hi", [P, TILES])
        f_lo = sb("f_lo", [P, TILES])
        tile1 = sb("tile1", [P, TILES, SLOTS])
        tok_u = sb("tok_u", [P, SLOTS], U32)
        past = sb("past", [P, SLOTS, NR])
        who = sb("who", [P, SLOTS])
        who_i = sb("who_i", [P, SLOTS], I32)
        s4 = sb("s4", [P, TILES])
        ps = ctx.enter_context(nc.psum_tensor("ps", [P, 8, 512], FP32))

        ident = cst[:, C_ID:C_ID + P]
        strict = cst[:, C_STRICT:C_STRICT + P]
        cum = cst[:, C_CUM:C_CUM + P]
        iota = cst[:, C_IOTA:C_IOTA + NE]
        before = cst[:, C_BEFORE:C_BEFORE + P]
        XC0 = DI + NH

        s_cst, s_vec, s_win, s_wout, s_small = (sem(n) for n in ("s_cst", "s_vec", "s_win", "s_wout", "s_small"))
        s_x = [sem(f"s_x{i}") for i in range(4)]
        s_wt = [sem(f"s_wt{t}") for t in range(KT)]
        s_w1, s_w2, s_wr = sem("s_w1"), sem("s_w2"), sem("s_wr")
        s_ones, s_wc, s_mult, s_sq = sem("s_ones"), sem("s_wc"), sem("s_mult"), sem("s_sq")
        s_sqd, s_tok = sem("s_sqd"), sem("s_tok")
        s_u, s_ut, s_utc = sem("s_u"), sem("s_ut"), sem("s_utc")
        s_xbc, s_z, s_cv0, s_cv, s_xs = (sem(n) for n in ("s_xbc", "s_z", "s_cv0", "s_cv", "s_xs"))
        s_dtx, s_sp, s_ea, s_zs, s_adt = (sem(n) for n in ("s_dtx", "s_sp", "s_ea", "s_zs", "s_adt"))
        s_segr, s_seg, s_E, s_gt, s_gtm = (sem(n) for n in ("s_segr", "s_seg", "s_E", "s_gt", "s_gtm"))
        s_xt, s_xtm, s_xD, s_xdt, s_M = (sem(n) for n in ("s_xt", "s_xtm", "s_xD", "s_xdt", "s_M"))
        s_y, s_yz, s_ss, s_yt, s_ytc, s_o = (sem(n) for n in ("s_y", "s_yz", "s_ss", "s_yt", "s_ytc", "s_o"))
        s_wo, s_u2, s_u2t, s_u2c, s_lg = (sem(n) for n in ("s_wo", "s_u2", "s_u2t", "s_u2c", "s_lg"))
        s_lgs, s_ex, s_coef, s_ct, s_ctc = (sem(n) for n in ("s_lgs", "s_ex", "s_coef", "s_ct", "s_ctc"))
        s_rows, s_oh, s_rank, s_where, s_tok1, s_idx, s_who = (sem(n) for n in (
            "s_rows", "s_oh", "s_rank", "s_where", "s_tok1", "s_idx", "s_who"))
        s_xg = [sem("s_xg0"), sem("s_xg1")]
        s_one, s_g, s_gc, s_l1, s_hg, s_ht, s_htd, s_hta = (sem(n) for n in (
            "s_one", "s_g", "s_gc", "s_l1", "s_hg", "s_ht", "s_htd", "s_hta"))
        s_l2, s_ys = sem("s_l2"), sem("s_ys")
        s_yw = [sem("s_yw0"), sem("s_yw1")]
        s_yt2 = [sem(f"s_yt2_{i}") for i in range(TILES)]
        s_b2o, s_hid, s_gel, s_eo, s_acc, s_out = (sem(n) for n in ("s_b2o", "s_hid", "s_gel", "s_eo", "s_acc", "s_out"))
        c_dve, c_act, c_pool = sem("c_dve"), sem("c_act"), sem("c_pool")

        block = ctx.enter_context(nc.Block())

        @block.sync
        def _(sp):
            sp.dma_start(vec[:], vec_d).then_inc(s_vec, 16)
            for t in range(KT):
                sp.dma_start(wtok[:, t], wtok_d[t]).then_inc(s_wt[t], 16)
            sp.dma_start(win[:], win_d).then_inc(s_win, 16)
            sp.dma_start(wout[:], wout_d).then_inc(s_wout, 16)
            sp.dma_start(ws[:], ws_d).then_inc(s_small, 16)
            sp.dma_start(b2[:], b2_d).then_inc(s_small, 16)
            sp.dma_start(w1[0:DH, 0], w1_d[0]).then_inc(s_w1, 16)
            sp.dma_start(w2[:, 0], w2_d[0]).then_inc(s_w2, 16)
            sp.dma_start(w1[DH:DH + 1, :, 1, :], b1_d).then_inc(s_wr, 16)
            for e in range(1, NE):
                sp.dma_start(w1[0:DH, e], w1_d[e]).then_inc(s_wr, 16)
                sp.dma_start(w2[:, e], w2_d[e]).then_inc(s_wr, 16)
            sp.wait_ge(s_u2, TILES)
            sp.dma_start(rows_d.rearrange("(i p) d -> p i d", p=P), u[:]).then_inc(s_rows, 16)
            for j in range(SLOTS):
                sp.wait_ge(s_ys, j + 1)
                sp.dma_start(sorted_d[j * P:(j + 1) * P, :], y_s[:, j % 2]).then_inc(s_yw[j % 2], 16)
            for i in range(TILES):
                sp.wait_ge(s_acc, TILES + i + 1)
                sp.dma_start(out_d[i * P:(i + 1) * P, :], h[:, i]).then_inc(s_out, 16)
            sp.wait_ge(s_out, 16 * TILES)

        @block.gpsimd
        def _(pool):
            pool.memset(ones[:], 1.0).then_inc(s_ones, 1)
            pool.wait_ge(s_vec, 16)
            pool.wait_ge(s_wout, 16)
            for c in range(DI // P):
                pool.tensor_scalar(wout[:, c], wout[:, c], vec[:, V_NW + c:V_NW + c + 1], None,
                                   ALU.mult).then_inc(s_wo, 1)
            pool.wait_ge(s_cst, 16)
            for i in range(TILES):
                pool.wait_ge(s_adt, 1)
                if i >= 2:
                    pool.wait_ge(s_seg, i - 1)
                a = adt[:, i, :].unsqueeze(2).to_broadcast([P, NH, P])
                c = cum.unsqueeze(1).to_broadcast([P, NH, P])
                pool.tensor_tensor(segr[:, i % 2], c, a, ALU.mult).then_inc(s_segr, 1)
            for i in range(TILES):
                pool.wait_ge(s_xtm, i + 1)
                dpar = vec[:, V_DPAR:V_DPAR + NH].unsqueeze(2).to_broadcast([P, NH, HD])
                x3 = x_tm[:, i].rearrange("p (h d) -> p h d", d=HD)
                o3 = xD[:, i].rearrange("p (h d) -> p h d", d=HD)
                pool.tensor_tensor(o3, x3, dpar, ALU.mult).then_inc(s_xD, 1)
            pool.wait_ge(s_rows, 16)
            pool.wait_ge(s_idx, 1)
            for j in range(SLOTS):
                if j >= 2:
                    pool.wait_ge(s_g, j - 1)
                pool.indirect_dma_start(xg[:, j % 2], None, rows_d,
                                        bass.IndirectOffsetOnAxis(ap=tok_u[:, j:j + 1], axis=0)).then_inc(s_xg[j % 2], 16)
            pool.wait_ge(s_yw[0], 16 * ((SLOTS + 1) // 2))
            pool.wait_ge(s_yw[1], 16 * (SLOTS // 2))
            for i in range(TILES):
                pool.indirect_dma_start(y_t[:, i], None, sorted_d,
                                        bass.IndirectOffsetOnAxis(ap=slot_u[:, i:i + 1], axis=0)).then_inc(s_yt2[i], 16)

        @block.scalar
        def _(act):
            done = [0]

            def link(ins):
                done[0] += 1
                ins.then_inc(c_act, 1)
                act.wait_ge(c_act, done[0])

            act.dma_start(cst[:], const_d).then_inc(s_cst, 16)
            for g in range(KT // 2):
                act.dma_start(xT[:, 2 * g:2 * g + 2], xT_d[:, 2 * g:2 * g + 2]).then_inc(s_x[g], 16)
            for t in range(KT):
                act.wait_ge(s_x[t // 2], 16)
                if t >= 2:
                    act.wait_ge(s_sqd, t - 1)
                act.activation(xT2[:, t % 2], xT[:, t], ACT.Square).then_inc(s_sq, 1)
            act.wait_ge(s_vec, 16)
            act.activation(ea[:], vec[:, V_ALOG:V_ALOG + NH], ACT.Exp).then_inc(s_ea, 1)
            act.wait_ge(s_ut, 2)
            act.activation(uT[:, 0], ps[0:DH, 5], ACT.Copy).then_inc(s_utc, 1)
            for n in range(NC4):
                c = (n + 3) % NC4
                act.wait_ge(s_xbc, n + 1)
                act.activation(acc[:, c], ps[:, c], ACT.Identity,
                               bias=vec[:, V_CB + c:V_CB + c + 1],
                               scale=vec[:, V_CW + c * TAPS + TAPS - 1:V_CW + c * TAPS + TAPS]).then_inc(s_cv0, 1)
            act.wait_ge(s_dtx, 1)
            link(act.activation(dta[:], dtx[:], ACT.Abs))
            link(act.activation(dta[:], dta[:], ACT.Exp, scale=-1.0))
            act.activation(dta[:], dta[:], ACT.Ln, bias=1.0).then_inc(s_sp, 1)
            for i in range(TILES):
                act.activation(zs[:, i], ps[:, 4 + i, 0:DI], ACT.Silu).then_inc(s_zs, 1)
            for n in range(NC4):
                c = (n + 3) % NC4
                act.wait_ge(s_cv, n + 1)
                if c == 3:
                    act.activation(Bt[0:DS, :], acc[0:DS, c], ACT.Silu).then_inc(s_xs, 1)
                    act.activation(Ct[0:DS, :], acc[DS:P, c], ACT.Silu).then_inc(s_xs, 1)
                else:
                    act.activation(xs[:, c], acc[:, c], ACT.Silu).then_inc(s_xs, 1)

            def decay(i):
                act.wait_ge(s_seg, i + 1)
                if i >= 2:
                    act.wait_ge(s_y, i - 1)
                b = 4 + 2 * (i % 2)
                act.activation(E[:, i % 2].rearrange("p (g h) l -> p g (h l)", g=2), ps[:, b:b + 2, 0:DI],
                               ACT.Exp).then_inc(s_E, 1)

            decay(0)
            decay(1)
            for i in range(TILES):
                act.wait_ge(s_xt, i + 1)
                act.activation(x_tm[:, i], ps[:, XB[i], 0:DI], ACT.Copy).then_inc(s_xtm, 1)
            decay(2)
            decay(3)
            for i in range(TILES):
                act.wait_ge(s_yz, i + 1)
                if i:
                    act.wait_ge(s_ss, i)
                act.activation(sq[:], x_tm[:, i], ACT.Square, accum_out=ss[:, i:i + 1]).then_inc(s_ss, 1)
                act.wait_ge(s_yt, i + 1)
                act.activation(yzT[:, i], ps[:, 4 + i, 0:DI], ACT.Copy).then_inc(s_ytc, 1)
            act.wait_ge(s_u2t, 2)
            act.activation(uT[:, 0], ps[0:DH, 4], ACT.Copy).then_inc(s_u2c, 1)
            act.wait_ge(s_lgs, 1)
            act.activation(ex[:], lg[:], ACT.Exp).then_inc(s_ex, 1)
            for f in range(FC):
                act.wait_ge(s_hid, f + 1)
                act.activation(hT[:, f], ps[:, f % 2], ACT.Gelu, bias=vec[:, V_B1 + f:V_B1 + f + 1]).then_inc(s_gel, 1)
            act.wait_ge(s_ct, 1)
            act.activation(coefT[:], ps[0:NE, 7], ACT.Copy).then_inc(s_ctc, 1)

            def hidden(j):
                act.wait_ge(s_l1, j + 1)
                if j >= 2:
                    act.wait_ge(s_ht, j - 1)
                act.activation(hid[:, j % 2].rearrange("p (g f) -> p g f", g=2),
                               ps[:, 2 * (j % 2):2 * (j % 2) + 2, 0:FH], ACT.Gelu).then_inc(s_hg, 1)

            def hidden_half(j):
                act.wait_ge(s_ht, j + 1)
                if j >= 2:
                    act.wait_ge(s_l2, j - 1)
                act.activation(hidT[:, j % 2, FH:FF], ps[:, 5, 0:FH], ACT.Copy).then_inc(s_hta, 1)

            hidden(0)
            for j in range(1, SLOTS):
                hidden(j)
                hidden_half(j - 1)
            hidden_half(SLOTS - 1)

        @block.vector
        def _(dve):
            done = [0]

            def link(ins):
                done[0] += 1
                ins.then_inc(c_dve, 1)
                dve.wait_ge(c_dve, done[0])

            def rsqrt(v, y):
                link(dve.tensor_scalar(rs_i[:], v.bitcast(I32), 1, None, ALU.logical_shift_right))
                link(dve.tensor_scalar(y.bitcast(I32), rs_i[:], -1.0, float(MAGIC), ALU.mult, ALU.add))
                for _ in range(3):
                    link(dve.tensor_tensor(rs_t[:], y, y, ALU.mult))
                    link(dve.tensor_tensor(rs_t[:], rs_t[:], v, ALU.mult))
                    link(dve.tensor_scalar(rs_t[:], rs_t[:], -0.5, 1.5, ALU.mult, ALU.add))
                    link(dve.tensor_tensor(y, y, rs_t[:], ALU.mult))

            def layernorm():
                for i in range(TILES):
                    link(dve.bn_stats(bns[:, i], h[:, i]))
                for i in range(TILES):
                    link(dve.bn_aggr(bna[:, i], bns[:, i]))
                link(dve.tensor_scalar(var[:], bna[:, :, 1], EPS, None, ALU.add))
                rsqrt(var[:], rs_y[:])
                link(dve.scalar_tensor_tensor(nmr[:], bna[:, :, 0], -1.0, rs_y[:], ALU.mult, ALU.mult))

            dve.wait_ge(s_cst, 16)
            dve.tensor_copy(wc[:, :, D], cst[:, C_MULT:C_MULT + KT]).then_inc(s_mult, 1)
            dve.wait_ge(s_vec, 16)
            for t in range(KT):
                dve.wait_ge(s_wt[t], 16)
                for s in range(SHIFTS):
                    g = vec[:, V_GAMMA + s * KT + t:V_GAMMA + s * KT + t + 1]
                    if s == 0:
                        link(dve.tensor_scalar(wc[:, t, 0:D], wtok[:, t, s], g, None, ALU.mult))
                    elif s < SHIFTS - 1:
                        link(dve.scalar_tensor_tensor(wc[:, t, 0:D], wtok[:, t, s], g, wc[:, t, 0:D], ALU.mult, ALU.add))
                    else:
                        dve.scalar_tensor_tensor(wc[:, t, 0:D], wtok[:, t, s], g, wc[:, t, 0:D],
                                                 ALU.mult, ALU.add).then_inc(s_wc, 1)
            dve.wait_ge(s_tok, 1)
            link(dve.tensor_copy(csc[:, 0:D], ps[:, 4, 0:D]))
            link(dve.tensor_tensor(csc[:, D:2 * D], ps[:, 4, D:2 * D], vec[:, V_TOKB:V_TOKB + D], ALU.add))
            link(dve.tensor_scalar(mv[:], ps[:, 0:TILES, D:D + 2], 1.0 / FEATS, None, ALU.mult))
            link(dve.tensor_tensor(var[:], mv[:, :, 0], mv[:, :, 0], ALU.mult))
            link(dve.tensor_tensor(var[:], mv[:, :, 1], var[:], ALU.subtract))
            link(dve.tensor_scalar(var[:], var[:], 0.0, EPS, ALU.max, ALU.add))
            rsqrt(var[:], rs_y[:])
            link(dve.scalar_tensor_tensor(nmr[:], mv[:, :, 0], -1.0, rs_y[:], ALU.mult, ALU.mult))
            for i in range(TILES):
                link(dve.scalar_tensor_tensor(h[:, i], csc[:, 0:D], nmr[:, i:i + 1], csc[:, D:2 * D], ALU.mult, ALU.add))
                link(dve.scalar_tensor_tensor(h[:, i], ps[:, i, 0:D], rs_y[:, i:i + 1], h[:, i], ALU.mult, ALU.add))
            layernorm()
            for i in range(TILES):
                dve.tensor_scalar(u[:, i], h[:, i], rs_y[:, i:i + 1], nmr[:, i:i + 1],
                                  ALU.mult, ALU.add).then_inc(s_u, 1)
            dve.wait_ge(s_ut, 2)
            dve.tensor_copy(uT[:, 1], ps[0:DH, 6]).then_inc(s_utc, 1)
            dve.wait_ge(s_z, TILES)
            dtb = vec[:, V_DTB:V_DTB + NH].unsqueeze(1).to_broadcast([P, TILES, NH])
            dve.tensor_tensor(dtx[:], ps[:, 4:8, DI:DI + NH], dtb, ALU.add).then_inc(s_dtx, 1)
            dve.wait_ge(s_sp, 1)
            dve.wait_ge(s_ea, 1)
            link(dve.scalar_tensor_tensor(dt[:], dtx[:], 0.0, dta[:], ALU.max, ALU.add))
            eab = ea[:].unsqueeze(1).to_broadcast([P, TILES, NH])
            dve.scalar_tensor_tensor(adt[:], dt[:], -1.0, eab, ALU.mult, ALU.mult).then_inc(s_adt, 1)
            for n in range(NC4):
                c = (n + 3) % NC4
                dve.wait_ge(s_cv0, n + 1)
                for k in range(1, TAPS):
                    w = vec[:, V_CW + c * TAPS + TAPS - 1 - k:V_CW + c * TAPS + TAPS - k]
                    a3 = acc[:, c].rearrange("p (b l) -> p b l", l=SEQ)[:, :, k:]
                    p3 = ps[:, c].rearrange("p (b l) -> p b l", l=SEQ)[:, :, 0:SEQ - k]
                    ins = dve.scalar_tensor_tensor(a3, p3, w, a3, ALU.mult, ALU.add)
                    if k < TAPS - 1:
                        link(ins)
                    else:
                        ins.then_inc(s_cv, 1)
            dve.wait_ge(s_gt, 1)
            cumb = cum.unsqueeze(1).to_broadcast([P, TILES, P])
            link(dve.tensor_tensor(GTm[:], ps[:, 3].rearrange("p (t l) -> p t l", l=P), cumb, ALU.mult))

            def mix(i):
                dve.wait_ge(s_E, i + 1)
                g = GTm[:, i].unsqueeze(1).to_broadcast([P, NH, P])
                dve.tensor_tensor(E[:, i % 2], E[:, i % 2], g, ALU.mult).then_inc(s_M, 1)
                dve.wait_ge(s_xtm, i + 1)
                x3 = x_tm[:, i].rearrange("p (h d) -> p h d", d=HD)
                o3 = xdt[:, i].rearrange("p (h d) -> p h d", d=HD)
                dve.tensor_tensor(o3, x3, dt[:, i].unsqueeze(2).to_broadcast([P, NH, HD]), ALU.mult).then_inc(s_xdt, 1)

            def gate(i):
                dve.wait_ge(s_y, i + 1)
                dve.wait_ge(s_xD, i + 1)
                link(dve.tensor_tensor(xD[:, i], ps[:, YB[i], 0:DI], xD[:, i], ALU.add))
                dve.wait_ge(s_zs, TILES)
                dve.tensor_tensor(x_tm[:, i], xD[:, i], zs[:, i], ALU.mult).then_inc(s_yz, 1)

            mix(0)
            mix(1)
            gate(0)
            mix(2)
            gate(1)
            mix(3)
            gate(2)
            gate(3)
            dve.wait_ge(s_ss, TILES)
            link(dve.tensor_scalar(var[:], ss[:], 1.0 / DI, EPS, ALU.mult, ALU.add))
            rsqrt(var[:], rs_y[:])
            for i in range(TILES):
                dve.wait_ge(s_o, i + 1)
                link(dve.scalar_tensor_tensor(h[:, i], ps[:, YB[i], 0:D], rs_y[:, i:i + 1], h[:, i], ALU.mult, ALU.add))
            layernorm()
            for i in range(TILES):
                dve.tensor_scalar(u[:, i], h[:, i], rs_y[:, i:i + 1], nmr[:, i:i + 1],
                                  ALU.mult, ALU.add).then_inc(s_u2, 1)
            dve.wait_ge(s_u2t, 2)
            dve.tensor_copy(uT[:, 1], ps[0:DH, 5]).then_inc(s_u2c, 1)
            dve.wait_ge(s_lg, 1)
            bsb = vec[:, V_BS:V_BS + NE].unsqueeze(1).to_broadcast([P, TILES, NE])
            iob = iota.unsqueeze(1).to_broadcast([P, TILES, NE])

            def wide(a):
                return a.unsqueeze(2).to_broadcast([P, TILES, NE])

            link(dve.tensor_tensor(lg[:], ps[:, 6, 0:TILES * NE].rearrange("p (t e) -> p t e", e=NE), bsb, ALU.add))
            link(dve.tensor_reduce(m4[:], lg[:], AX.X, ALU.max))
            dve.tensor_tensor(lg[:], lg[:], wide(m4[:]), ALU.subtract).then_inc(s_lgs, 1)
            dve.wait_ge(s_lgs, 1)
            link(dve.tensor_scalar(oh[:], lg[:], 0.0, -float(NE), ALU.is_equal, ALU.mult))
            link(dve.tensor_tensor(oh[:], oh[:], iob, ALU.add))
            link(dve.tensor_reduce(m4[:], oh[:], AX.X, ALU.min))
            link(dve.tensor_scalar(m4[:], m4[:], float(NE), None, ALU.add))
            dve.tensor_tensor(oh[:], iob, wide(m4[:]), ALU.is_equal).then_inc(s_oh, 1)
            dve.wait_ge(s_rank, 1)
            link(dve.tensor_copy(cnt[:], ps[:, 6, 0:2 * TILES * NR].rearrange("p (a t e) -> p a t e", a=2, e=NR)))
            link(dve.tensor_reduce(tot[:], cnt[:, 1].rearrange("p t e -> p e t"), AX.X, ALU.add))
            totb = tot[:].unsqueeze(2).to_broadcast([P, NR, TILES])
            full = iota[:, 0:TILES].unsqueeze(1).to_broadcast([P, NR, TILES])
            link(dve.tensor_scalar(tot[:], tot[:], 1.0 / P, None, ALU.mult))
            link(dve.tensor_tensor(more[:], totb, full, ALU.is_gt))
            link(dve.tensor_reduce(need[:], more[:], AX.X, ALU.add))
            link(dve.tensor_tensor_scan(end[:], ones[:, 0:NR], need[:], 0.0, ALU.mult, ALU.add))
            link(dve.tensor_tensor(base[:, 0], end[:], need[:], ALU.subtract))
            link(dve.tensor_scalar(base[:, 0], base[:, 0], float(P), None, ALU.mult))
            for i in range(1, TILES):
                link(dve.tensor_tensor(base[:, i], base[:, i - 1], cnt[:, 1, i - 1], ALU.add))
            link(dve.tensor_tensor(base[:], base[:], cnt[:, 0], ALU.add))
            link(dve.tensor_tensor(base[:], base[:], oh[:, :, 1:NE], ALU.mult))
            link(dve.tensor_reduce(slot[:], base[:], AX.X, ALU.add))
            link(dve.tensor_copy(slot_u[:], slot[:]))
            link(dve.tensor_scalar(s_hi[:], slot_u[:].bitcast(I32), 7, None, ALU.arith_shift_right))
            link(dve.tensor_scalar(s_lo[:], slot_u[:].bitcast(I32), P - 1, None, ALU.bitwise_and))
            link(dve.tensor_copy(f_lo[:], s_lo[:]))
            link(dve.scalar_tensor_tensor(f_hi[:], oh[:, :, 0], float(SLOTS + 1), s_hi[:], ALU.mult, ALU.add))
            io_s = cst[:, C_IOTA:C_IOTA + SLOTS].unsqueeze(1).to_broadcast([P, TILES, SLOTS])
            link(dve.tensor_tensor(tile1[:], io_s, f_hi[:].unsqueeze(2).to_broadcast([P, TILES, SLOTS]), ALU.is_equal))
            for i in range(TILES):
                link(dve.tensor_scalar(tile1[:, i], tile1[:, i], cst[:, C_TOK + i:C_TOK + i + 1], None, ALU.mult))
            for i in range(TILES):
                dve.tensor_scalar(pos1[:, i], cst[:, C_LANE:C_LANE + P], f_lo[:, i:i + 1], None,
                                  ALU.is_equal).then_inc(s_where, 1)
            dve.wait_ge(s_tok1, 1)
            dve.tensor_copy(tok_u[:], ps[:, 6, 128:128 + SLOTS]).then_inc(s_idx, 1)
            io_n = cst[:, C_IOTA:C_IOTA + SLOTS].unsqueeze(2).to_broadcast([P, SLOTS, NR])
            link(dve.tensor_tensor(past[:], io_n, end[:].unsqueeze(1).to_broadcast([P, SLOTS, NR]), ALU.is_ge))
            link(dve.tensor_reduce(who[:], past[:], AX.X, ALU.add))
            dve.tensor_scalar(who_i[:], who[:], 1.0, float(NR), ALU.add, ALU.min).then_inc(s_who, 1)
            dve.wait_ge(s_ex, 1)
            link(dve.tensor_reduce(s4[:], ex[:], AX.X, ALU.add))
            link(dve.reciprocal(p4[:], s4[:]))
            link(dve.tensor_tensor(coef[:], oh[:], wide(p4[:]), ALU.mult))
            link(dve.tensor_scalar(s4[:], p4[:], -1.0, 1.0, ALU.mult, ALU.add))
            dve.tensor_tensor(coef[:, :, 0], coef[:, :, 0], s4[:], ALU.add).then_inc(s_coef, 1)
            link(dve.tensor_tensor(gate_sel[:], p4[:], oh[:, :, 0], ALU.mult))
            link(dve.tensor_tensor(gate_sel[:], p4[:], gate_sel[:], ALU.subtract))
            for i in range(TILES):
                dve.wait_ge(s_eo, i + 1)
                link(dve.scalar_tensor_tensor(h[:, i], ps[:, 2 + i, 0:D], coef[:, i, 0:1], h[:, i],
                                              ALU.mult, ALU.add))
            for i in range(TILES):
                dve.wait_ge(s_b2o, i + 1)
                dve.tensor_tensor(h[:, i], h[:, i], ps[:, i % 2, 0:D], ALU.add).then_inc(s_acc, 1)

            def gathered(j):
                dve.wait_ge(s_g, j + 1)
                if j >= 2:
                    dve.wait_ge(s_l1, j - 1)
                dve.tensor_copy(xgT[0:DH, j % 2], ps[0:DH, 7, 0:2 * P].rearrange("p (k t) -> p k t", k=2)).then_inc(s_gc, 1)

            def hidden_half(j):
                dve.wait_ge(s_ht, j + 1)
                if j >= 2:
                    dve.wait_ge(s_l2, j - 1)
                dve.tensor_copy(hidT[:, j % 2, 0:FH], ps[:, 4, 0:FH]).then_inc(s_htd, 1)

            def result(j):
                dve.wait_ge(s_l2, j + 1)
                if j >= 2:
                    dve.wait_ge(s_yw[j % 2], 16 * (j // 2))
                dve.tensor_copy(y_s[:, j % 2], ps[:, 6, 0:D]).then_inc(s_ys, 1)

            dve.tensor_copy(xgT[DH:DH + 1, :, 1], ones[DH:DH + 1].unsqueeze(1).to_broadcast([1, 2, P])).then_inc(s_one, 1)
            gathered(0)
            for j in range(SLOTS + 2):
                if j + 1 < SLOTS:
                    gathered(j + 1)
                if 1 <= j <= SLOTS:
                    hidden_half(j - 1)
                if j >= 2:
                    result(j - 2)
            for i in range(TILES):
                dve.wait_ge(s_yt2[i], 16)
                dve.wait_ge(s_acc, TILES)
                dve.scalar_tensor_tensor(h[:, i], y_t[:, i], gate_sel[:, i:i + 1], h[:, i],
                                         ALU.mult, ALU.add).then_inc(s_acc, 1)

        @block.tensor
        def _(pe):
            mm = pe.matmul
            pe.wait_ge(s_ones, 1)
            pe.wait_ge(s_vec, 16)
            pe.wait_ge(s_mult, 1)
            for t in range(KT):
                pe.wait_ge(s_wt[t], 16)
                for s in range(SHIFTS):
                    b = vec[:, V_BETA + s * KT + t:V_BETA + s * KT + t + 1].to_broadcast([P, P])
                    mm(ps[:, 4, D:2 * D], b, wtok[:, t, s], start=(t == 0 and s == 0),
                       stop=(t == KT - 1 and s == SHIFTS - 1), skip_group_check=True)
                pe.wait_ge(s_wc, t + 1)
                mm(ps[:, 4, 0:D], ones[:], wc[:, t, 0:D], start=False, stop=(t == KT - 1), skip_group_check=True)
                pe.wait_ge(s_x[t // 2], 16)
                for i in range(TILES):
                    mm(ps[:, i, 0:D + 1], xT[:, t, i * P:(i + 1) * P], wc[:, t], start=(t == 0),
                       stop=(t == KT - 1), skip_group_check=True)
                pe.wait_ge(s_sq, t + 1)
                for i in range(TILES):
                    last = mm(ps[:, i, D + 1:D + 2], xT2[:, t % 2, i * P:(i + 1) * P], wc[:, t, D:D + 1],
                              start=False, stop=(t == KT - 1), skip_group_check=True)
                last.then_inc(s_sqd, 1)
                if t == KT - 1:
                    mm(ps[:, 7, 0:1], ones[:, :], ones[:, 0:1], start=True, stop=True).then_inc(s_tok, 1)

            def turn(src, produced, banks, turned):
                for i in range(TILES):
                    pe.wait_ge(produced, i + 1)
                    for k in range(2):
                        last = pe.transpose(ps[0:DH, banks[k], i * P:(i + 1) * P],
                                            src[:, i, k * DH:(k + 1) * DH], ident)
                last.then_inc(turned, 2)

            pe.wait_ge(s_cst, 16)
            turn(u, s_u, (5, 6), s_ut)
            pe.wait_ge(s_utc, 2)
            pe.wait_ge(s_win, 16)
            for n in range(NC4):
                c = (n + 3) % NC4
                for k in range(2):
                    last = mm(ps[:, c], win[:, k, XC0 + c * P:XC0 + (c + 1) * P], uT[:, k],
                              start=(k == 0), stop=(k == 1))
                last.then_inc(s_xbc, 1)
            for i in range(TILES):
                for k in range(2):
                    last = mm(ps[:, 4 + i, 0:XC0], uT[:, k, i * P:(i + 1) * P], win[:, k, 0:XC0],
                              start=(k == 0), stop=(k == 1))
                last.then_inc(s_z, 1)

            def segments(i):
                pe.wait_ge(s_segr, i + 1)
                pe.wait_ge(s_zs, TILES)
                if i >= 2:
                    pe.wait_ge(s_E, i - 1)
                for g in range(2):
                    last = mm(ps[:, 4 + 2 * (i % 2) + g, 0:DI], strict,
                              segr[:, i % 2, 3 * g:3 * g + 3].rearrange("p h l -> p (h l)"), start=True, stop=True)
                last.then_inc(s_seg, 1)

            def ssd(i):
                pe.wait_ge(s_M, i + 1)
                pe.wait_ge(s_xdt, i + 1)
                pe.wait_ge(s_xtm, TILES)
                for n in range(NH):
                    last = mm(ps[:, YB[i], n * HD:(n + 1) * HD], E[:, i % 2, n], xdt[:, i, n * HD:(n + 1) * HD],
                              start=True, stop=True)
                last.then_inc(s_y, 1)

            def turn_y(i):
                pe.wait_ge(s_yz, i + 1)
                pe.wait_ge(s_E, 3 if i < 2 else 4)
                for c in range(DI // P):
                    last = pe.transpose(ps[:, 4 + i, c * P:(c + 1) * P], x_tm[:, i, c * P:(c + 1) * P], ident)
                last.then_inc(s_yt, 1)

            pe.wait_ge(s_xs, 2)
            for i in range(TILES):
                r = slice(i * P, (i + 1) * P)
                last = mm(ps[:, 3, r], Bt[0:DS, r], Ct[0:DS, r], start=True, stop=True)
            last.then_inc(s_gt, 1)
            segments(0)
            segments(1)
            pe.wait_ge(s_xs, NC4 + 1)
            for i in range(TILES):
                if i == 3:
                    pe.wait_ge(s_xtm, 1)
                for c in range(DI // P):
                    last = pe.transpose(ps[:, XB[i], c * P:(c + 1) * P], xs[:, c, i * P:(i + 1) * P], ident)
                last.then_inc(s_xt, 1)
            ssd(0)
            segments(2)
            ssd(1)
            segments(3)
            turn_y(0)
            ssd(2)
            turn_y(1)
            ssd(3)
            turn_y(2)
            turn_y(3)
            pe.wait_ge(s_wo, DI // P)
            for i in range(TILES):
                pe.wait_ge(s_ytc, i + 1)
                for c in range(DI // P):
                    last = mm(ps[:, YB[i], 0:D], yzT[:, i, c * P:(c + 1) * P], wout[:, c],
                              start=(c == 0), stop=(c == DI // P - 1))
                last.then_inc(s_o, 1)
            turn(u, s_u2, (4, 5), s_u2t)
            pe.wait_ge(s_u2c, 2)
            pe.wait_ge(s_small, 32)
            for i in range(TILES):
                for k in range(2):
                    last = mm(ps[:, 6, i * NE:(i + 1) * NE], uT[:, k, i * P:(i + 1) * P], ws[:, k],
                              start=(k == 0), stop=(k == 1))
            last.then_inc(s_lg, 1)
            pe.wait_ge(s_w1, 16)

            def hidden0(f):
                if f >= 2:
                    pe.wait_ge(s_gel, f - 1)
                for k in range(2):
                    last = mm(ps[:, f % 2], w1[0:DH, 0, k, f * P:(f + 1) * P], uT[:, k], start=(k == 0), stop=(k == 1))
                last.then_inc(s_hid, 1)

            hidden0(0)
            hidden0(1)
            pe.wait_ge(s_oh, 1)
            mm(ps[:, 6, 0:TILES * NR], before, oh[:, :, 1:NE], start=True, stop=True)
            mm(ps[:, 6, TILES * NR:2 * TILES * NR], ones[:], oh[:, :, 1:NE], start=True, stop=True).then_inc(s_rank, 1)
            for f in range(2, FC):
                hidden0(f)
            pe.wait_ge(s_where, TILES)
            for i in range(TILES):
                last = mm(ps[:, 6, 128:128 + SLOTS], pos1[:, i], tile1[:, i], start=(i == 0), stop=(i == TILES - 1))
            last.then_inc(s_tok1, 1)
            pe.wait_ge(s_coef, 1)
            for i in range(TILES):
                last = pe.transpose(ps[0:NE, 7, i * P:(i + 1) * P], coef[:, i], ident)
            last.then_inc(s_ct, 1)
            pe.wait_ge(s_w2, 16)
            for i in range(TILES):
                for f in range(FC):
                    if i == 0:
                        pe.wait_ge(s_gel, f + 1)
                    last = mm(ps[:, 2 + i, 0:D], hT[:, f, i * P:(i + 1) * P], w2[:, 0, f],
                              start=(f == 0), stop=(f == FC - 1))
                last.then_inc(s_eo, 1)
            pe.wait_ge(s_ctc, 1)
            pe.wait_ge(s_gel, FC)
            for i in range(TILES):
                if i >= 2:
                    pe.wait_ge(s_acc, i - 1)
                mm(ps[:, i % 2, 0:D], coefT[:, i * P:(i + 1) * P], b2[:], start=True, stop=True).then_inc(s_b2o, 1)

            def turn_rows(j):
                pe.wait_ge(s_xg[j % 2], 16 * (j // 2 + 1))
                if j:
                    pe.wait_ge(s_gc, j)
                for k in range(2):
                    last = pe.transpose(ps[0:DH, 7, k * P:(k + 1) * P], xg[:, j % 2, k * DH:(k + 1) * DH], ident)
                last.then_inc(s_g, 1)

            def hidden(j):
                e = pe.value_load(who_i[0:1, j:j + 1], min_val=1, max_val=NR)
                pe.wait_ge(s_gc, j + 1)
                if j >= 2:
                    pe.wait_ge(s_hg, j - 1)
                for g in range(2):
                    for k in range(2):
                        last = mm(ps[:, 2 * (j % 2) + g, 0:FH], xgT[0:DH + k, j % 2, k],
                                  w1[0:DH + k, bass.ds(e, 1), k, g * FH:(g + 1) * FH], start=(k == 0), stop=(k == 1))
                last.then_inc(s_l1, 1)

            def turn_hidden(j):
                pe.wait_ge(s_hg, j + 1)
                if j:
                    pe.wait_ge(s_htd, j)
                    pe.wait_ge(s_hta, j)
                for f in range(FC):
                    last = pe.transpose(ps[:, 4 + f // 3, f % 3 * P:(f % 3 + 1) * P], hid[:, j % 2, f * P:(f + 1) * P], ident)
                last.then_inc(s_ht, 1)

            def down(j):
                e = pe.value_load(who_i[0:1, j:j + 1], min_val=1, max_val=NR)
                pe.wait_ge(s_htd, j + 1)
                pe.wait_ge(s_hta, j + 1)
                if j:
                    pe.wait_ge(s_ys, j)
                for f in range(FC):
                    last = mm(ps[:, 6, 0:D], hidT[:, j % 2, f * P:(f + 1) * P], w2[:, bass.ds(e, 1), f],
                              start=(f == 0), stop=(f == FC - 1))
                last.then_inc(s_l2, 1)

            pe.wait_ge(s_who, 1)
            pe.wait_ge(s_wr, 16 * (2 * NR + 1))
            pe.wait_ge(s_one, 1)
            pe.wait_ge(s_acc, TILES)
            turn_rows(0)
            for j in range(SLOTS + 2):
                if j + 1 < SLOTS:
                    turn_rows(j + 1)
                if j < SLOTS:
                    hidden(j)
                if 1 <= j <= SLOTS:
                    turn_hidden(j - 1)
                if j >= 2:
                    down(j - 2)


def kernel(**inputs):
    import numpy as np
    import concourse.bacc as bacc
    from concourse.bass_utils import run_bass_kernel_spmd

    a = {k: np.asarray(v) for k, v in inputs.items()}

    def wrap(rows):
        full = np.zeros((KT * P,) + rows.shape[1:], rows.dtype)
        full[:rows.shape[0]] = rows
        return np.moveaxis(full.reshape((KT, P) + rows.shape[1:]), 1, 0)

    xp = np.pad(a["x"], ((0, 0), (0, 0), (1, 1), (1, 1)))
    n = a["x"].shape[2] // PATCH
    cut = np.stack([xp[:, :, PATCH * i:PATCH * i + EXT, PATCH * j:PATCH * j + EXT]
                    for i in range(n) for j in range(n)], 1)
    xT = wrap(cut.transpose(3, 2, 4, 0, 1).reshape(EXT * CH * EXT, TOKENS))

    offset = [(1, 1), (1, 0), (1, 2), (0, 1), (2, 1)]

    def spread(v):
        v = v.reshape((PATCH, PATCH, SHIFTS, CH) + v.shape[1:])
        out = np.zeros((SHIFTS, EXT, CH, EXT) + v.shape[4:], v.dtype)
        for s, (r, c) in enumerate(offset):
            out[s, r:r + PATCH, :, c:c + PATCH] = np.swapaxes(v[:, :, s], 1, 2)
        out = np.moveaxis(out, 0, 3)
        return wrap(out.reshape((EXT * CH * EXT, SHIFTS) + v.shape[4:]))

    wtok = np.ascontiguousarray(spread(a["L0_tok_W"]).swapaxes(0, 1))
    gamma = spread(a["L0_tok_gamma"]).transpose(0, 2, 1).reshape(P, SHIFTS * KT)
    beta = spread(a["L0_tok_beta"]).transpose(0, 2, 1).reshape(P, SHIFTS * KT)

    def rows(v):
        return np.broadcast_to(v.reshape(1, -1), (P, v.size))

    def cols(v):
        v = v.reshape(-1, P, v.size // v.shape[0])
        return v.transpose(1, 0, 2).reshape(P, -1)

    vec = np.concatenate([gamma, beta, rows(a["L0_tok_b"]),
                          cols(a["L0_attn_conv_w"].reshape(-1, TAPS)), cols(a["L0_attn_conv_b"]),
                          rows(a["L0_attn_dt_bias"]), rows(a["L0_attn_A_log"]), rows(a["L0_attn_D_param"]),
                          cols(a["L0_attn_norm_w"]), rows(a["L0_ffn_bs"]), cols(a["L0_ffn_b1"][0])], 1)
    w_in = a["L0_attn_W_in"].T
    z_end, xbc_end = DI, DI + DI + 2 * DS
    win = np.concatenate([w_in[:, :z_end], w_in[:, xbc_end:], w_in[:, z_end:xbc_end]], 1)
    win = win.reshape(2, DH, -1).transpose(1, 0, 2)
    wout = a["L0_attn_W_out"].T.reshape(DI // P, P, D).transpose(1, 0, 2)
    ws = a["L0_ffn_Ws"].reshape(2, DH, NE).transpose(1, 0, 2)
    w1 = a["L0_ffn_W1"].reshape(NE, 2, DH, FF).transpose(0, 2, 1, 3)
    w2 = a["L0_ffn_W2"].reshape(NE, FC, P, D).transpose(0, 2, 1, 3)

    k, m = np.arange(P)[:, None], np.arange(P)[None, :]
    same = k // SEQ == m // SEQ
    seen = np.zeros((EXT, CH, EXT), np.float32)
    for r, c in offset:
        seen[r:r + PATCH, :, c:c + PATCH] += 1
    const = np.concatenate([k == m, same & (k > m), same & (k <= m), wrap(seen.reshape(-1)),
                            np.broadcast_to(np.arange(16), (P, 16)), k < m,
                            np.broadcast_to(m, (P, P)), k + P * np.arange(TILES)[None, :]], 1).astype(np.float32)

    data = dict(xT=xT, wtok=wtok, const=const, vec=vec, win=win, wout=wout, ws=ws, b2=a["L0_ffn_b2"],
                b1=a["L0_ffn_b1"].reshape(1, NE, FF), w1=w1, w2=w2)
    nc = bacc.Bacc("TRN2", target_bir_lowering=False, num_devices=1)
    arrays, args = {}, []
    for name, v in data.items():
        arrays[name + "_dram"] = np.ascontiguousarray(v)
        args.append(nc.dram_tensor(name + "_dram", v.shape, mybir.dt.from_np(v.dtype), kind="ExternalInput").ap())
    args.append(nc.dram_tensor("expert_rows", (TOKENS, D), FP32, kind="Internal").ap())
    args.append(nc.dram_tensor("sorted_results", (SLOTS * P, D), FP32, kind="Internal").ap())
    args.append(nc.dram_tensor("out", (TOKENS, D), FP32, kind="ExternalOutput").ap())
    vit_tower(nc, *args)
    r = run_bass_kernel_spmd(nc, [arrays], core_ids=[0])
    return r.results[0]["out"].reshape(IMGS, SEQ, D)
```

```python
import concourse.bass as bass
from concourse import mybir
from contextlib import ExitStack

FP32 = mybir.dt.float32
I32 = mybir.dt.int32
U32 = mybir.dt.uint32
ALU = mybir.AluOpType
ACT = mybir.ActivationFunctionType
AX = mybir.AxisListType

P = 128
TOKENS, D = 512, 192
TILES = TOKENS // P
IMGS, SEQ = 8, 64
HALF = (slice(0, TOKENS // 2), slice(TOKENS // 2, TOKENS))
PATCH, CH = 16, 3
SHIFTS = 5
FEATS = PATCH * PATCH * CH * SHIFTS
EXT = PATCH + 2
KT = 8
QUADS = 4
QW = P // QUADS
DH = D // 2
DI, DS, NH, HD = 384, 64, 6, 64
NC4 = (DI + 2 * DS) // P
TAPS = 4
XB = (0, 1, 2, 0)
YB = (3, 1, 2, 0)
NE, FF = 9, 768
NR = NE - 1
FC = FF // P
FH = FF // 2
KB = D - P
OVER = (TOKENS - 1) // P
SLOTS = NR + OVER
STEPS = TILES + NR
WARM = (4, 5, 3, 3)
EPS = 1e-5

C_ID, C_STRICT, C_CUM = 0, P, 2 * P
C_IOTA = C_CUM + SEQ
C_BEFORE = C_IOTA + 16
C_LANE = C_BEFORE + P
C_TOK = C_LANE + P
C_N = C_TOK + TILES + 1
V_GAMMA, V_BETA = 0, SHIFTS * KT
V_TOKB = 2 * SHIFTS * KT
V_CW = V_TOKB + D
V_CB = V_CW + NC4 * TAPS
V_DTB = V_CB + NC4
V_ALOG = V_DTB + NH
V_DPAR = V_ALOG + NH
V_NW = V_DPAR + NH
V_BS = V_NW + DI // P
V_MULT = V_BS + NE
V_N = V_MULT + KT


def vit_tower(nc, xT_d, wtok_d, const_d, vec_d, win_d, wout_d, ws_d, b2_d, w1a_d, w1b_d, w2_d, rows_d, base_d, out_d):
    ctx = ExitStack()
    with ctx:
        def sb(name, shape, dt=FP32):
            return ctx.enter_context(nc.sbuf_tensor(name, shape, dt))

        def sem(name):
            return ctx.enter_context(nc.semaphore(name))

        cst = sb("cst", [P, C_N])
        vec = sb("vec", [P, V_N])
        win = sb("win", [DH, 2, 2 * DI + 2 * DS + NH])
        wout = sb("wout", [P, DI // P, D])
        ws = sb("ws", [P, 2, QW])
        b2 = sb("b2", [NE, D])
        w1 = sb("w1", [P, NE, 2, FF])
        w2 = sb("w2", [P, NE, FC, D])
        xr = sb("xr", [P, 2, 2, P])
        ones = sb("ones", [P, P])
        mean = sb("mean", [P, P])
        part = sb("part", [P, 2 * D])
        partx = sb("partx", [P, TOKENS])
        arena = sb("arena", [P, 17800])
        place = [0]

        def view(*dims):
            n = 1
            for d in dims:
                n *= d
            a = arena[:, place[0]:place[0] + n]
            place[0] += n
            if len(dims) == 2:
                a = a.rearrange("p (a b) -> p a b", b=dims[1])
            if len(dims) == 3:
                a = a.rearrange("p (a b c) -> p a b c", b=dims[1], c=dims[2])
            return a

        wtok = view(KT, SHIFTS, D)
        xT = view(KT, TOKENS)
        wc = view(KT, D + 1)
        xT2 = view(KT, TOKENS)
        csc = view(2 * D)
        place[0] = 0
        acc = view(NC4, TOKENS)
        yzT = acc[:, 0:3].rearrange("p a b -> p (a b)").rearrange("p (t c) -> p t c", c=DI)
        Ct = view(TOKENS)
        zs = view(TILES, DI)
        segr = view(TILES, DI)
        E = view(TILES, DI)
        x_tm = view(TILES, DI)
        xdt = view(TILES, DI)
        xD = view(TILES, DI)
        GTm = view(TILES, SEQ)
        M = view(TILES, NH * P).rearrange("p t (h l) -> p t h l", l=P)
        place[0] = 0
        hT = view(2, FF)
        xg = view(NR, D)
        y_s = view(4, D)
        hb = view(4, D + 1)
        pos1 = view(TILES, P)
        coefT = view(TOKENS)[0:NE]

        h = sb("h", [P, TILES, D + 2])
        u = sb("u", [P, TILES, D])
        uT = sb("uT", [P, 2, TOKENS])
        neg_mean = sb("neg_mean", [P, TILES])
        square = sb("square", [P, TILES])
        bns = sb("bns", [P, TILES, 6])
        bna = sb("bna", [P, TILES, 2])
        var = sb("var", [P, TILES])
        eps = sb("eps", [P, 1])
        rstd = sb("rstd", [P, TILES])
        table_out = sb("table_out", [P, 1])
        root_t = sb("root_t", [P, TILES])
        dtx = sb("dtx", [P, TILES, NH])
        dta = sb("dta", [P, TILES, NH])
        dt = sb("dt", [P, TILES, NH])
        adt = sb("adt", [P, TILES, NH])
        ea = sb("ea", [P, NH])
        ss = sb("ss", [P, TILES])
        lg = sb("lg", [P, TILES, NE])
        ex = sb("ex", [P, TILES, NE])
        oh = sb("oh", [P, TILES, NE])
        coef = sb("coef", [P, TILES, NE])
        m4 = sb("m4", [P, TILES])
        p4 = sb("p4", [P, TILES])
        gate_first = sb("gate_first", [P, TILES])
        cnt = sb("cnt", [P, 2, TILES, NR])
        tot = sb("tot", [P, NR])
        more = sb("more", [P, NR, OVER])
        need = sb("need", [P, NR])
        end = sb("end", [P, NR])
        shift = sb("shift", [P, NR])
        rank = sb("rank", [P, 2, TILES])
        slot = sb("slot", [P, TILES])
        slot_u = sb("slot_u", [P, TILES], U32)
        slot_hi = sb("slot_hi", [P, TILES], I32)
        slot_lo = sb("slot_lo", [P, TILES], I32)
        f_hi = sb("f_hi", [P, TILES])
        f_lo = sb("f_lo", [P, TILES])
        tile1 = sb("tile1", [P, TILES, SLOTS])
        tok_u = sb("tok_u", [P, SLOTS], U32)
        tok_w = sb("tok_w", [P, SLOTS], U32)
        tok_f = sb("tok_f", [P, SLOTS])
        past = sb("past", [P, OVER, NR])
        who = sb("who", [P, OVER])
        who_i = sb("who_i", [P, OVER + 1], I32)
        s4 = sb("s4", [P, TILES])
        ps = ctx.enter_context(nc.psum_tensor("ps", [P, 8, 512], FP32))

        ident = cst[:, C_ID:C_ID + P]
        strict = cst[:, C_STRICT:C_STRICT + P]
        cum = cst[:, C_CUM:C_CUM + SEQ]
        iota = cst[:, C_IOTA:C_IOTA + NE]
        before = cst[:, C_BEFORE:C_BEFORE + P]
        XC0 = DI + NH

        consts_loaded = sem("consts_loaded")
        vec_loaded = sem("vec_loaded")
        x_loaded = [sem(f"x_loaded{i}") for i in range(KT // 2)]
        wtok_loaded = [sem(f"wtok_loaded{i}") for i in range(KT)]
        win_loaded = sem("win_loaded")
        wout_loaded = sem("wout_loaded")
        router_loaded = sem("router_loaded")
        expert_loaded = [sem(f"expert_loaded{i}") for i in range(NE)]
        overflow_loaded = sem("overflow_loaded")
        ones_set = sem("ones_set")
        eps_set = sem("eps_set")
        mean_set = sem("mean_set")
        ones_row_set = sem("ones_row_set")
        wout_scaled = sem("wout_scaled")
        M_blanked = sem("M_blanked")
        seen_ready = sem("seen_ready")
        first_shift_ready = sem("first_shift_ready")
        wc_ready = sem("wc_ready")
        squares_ready = sem("squares_ready")
        squares_added = sem("squares_added")
        token_squares_ready = sem("token_squares_ready")
        tile_sums_ready = sem("tile_sums_ready")
        tile_sums_copied = sem("tile_sums_copied")
        sums_ready = sem("sums_ready")
        csc_ready = sem("csc_ready")
        projected = sem("projected")
        centred_ready = sem("centred_ready")
        h_ready = sem("h_ready")
        bn_stats_ready = sem("bn_stats_ready")
        var_ready = sem("var_ready")
        root_ready = sem("root_ready")
        u_ready = sem("u_ready")
        u_turned = sem("u_turned")
        uT_ready = [sem(f"uT_ready{i}") for i in range(2)]
        xbc_ready = sem("xbc_ready")
        last_tap_ready = sem("last_tap_ready")
        conv_ready = sem("conv_ready")
        conv_silu_ready = sem("conv_silu_ready")
        dt_projected = sem("dt_projected")
        dt_copied = sem("dt_copied")
        dt_turned = sem("dt_turned")
        z_ready = sem("z_ready")
        zs_ready = sem("zs_ready")
        dt_biased = sem("dt_biased")
        softplus_ready = sem("softplus_ready")
        a_ready = sem("a_ready")
        adt_ready = sem("adt_ready")
        stairs_ready = sem("stairs_ready")
        seg_ready = sem("seg_ready")
        decay_ready = sem("decay_ready")
        cb_ready = sem("cb_ready")
        cb_masked = sem("cb_masked")
        x_turned = sem("x_turned")
        x_tm_ready = [sem(f"x_tm_ready{i}") for i in range(2)]
        xdt_ready = sem("xdt_ready")
        xD_ready = sem("xD_ready")
        M_ready = sem("M_ready")
        y_ready = sem("y_ready")
        skip_added = sem("skip_added")
        y_gated = sem("y_gated")
        y_squared = sem("y_squared")
        y_turned = sem("y_turned")
        yT_ready = sem("yT_ready")
        out_projected = sem("out_projected")
        u2_ready = sem("u2_ready")
        u2_turned = sem("u2_turned")
        u2T_ready = [sem(f"u2T_ready{i}") for i in range(2)]
        logits_projected = sem("logits_projected")
        logits_copied = sem("logits_copied")
        logits_ready = sem("logits_ready")
        logits_less_max = sem("logits_less_max")
        exp_ready = sem("exp_ready")
        choice_ready = sem("choice_ready")
        shares_ready = sem("shares_ready")
        shares_turned = sem("shares_turned")
        coefT_ready = sem("coefT_ready")
        ranks_ready = sem("ranks_ready")
        slots_ready = sem("slots_ready")
        slot_tokens_ready = sem("slot_tokens_ready")
        indices_ready = sem("indices_ready")
        overflow_known = sem("overflow_known")
        rows_stored = sem("rows_stored")
        base_stored = sem("base_stored")
        out_stored = sem("out_stored")
        rows_gathered = [sem(f"rows_gathered{i}") for i in range(NR)]
        base_gathered = [sem(f"base_gathered{i}") for i in range(4)]
        scattered = [sem(f"scattered{i}") for i in range(4)]
        rows_turned = sem("rows_turned")
        rowsT_ready = sem("rowsT_ready")
        hidden_ready = sem("hidden_ready")
        gelu_ready = sem("gelu_ready")
        down_ready = sem("down_ready")
        result_ready = sem("result_ready")
        biases_ready = sem("biases_ready")
        biases_added = sem("biases_added")
        dve_done = sem("dve_done")
        act_done = sem("act_done")

        def expert(s):
            return s - TILES + 1 if TILES <= s < STEPS else 0

        def l1_banks(s):
            return slice(2 * (s % 2), 2 * (s % 2) + 2)

        block = ctx.enter_context(nc.Block())

        @block.sync
        def _(sp):
            sp.dma_start(vec[:], vec_d).then_inc(vec_loaded, 16)
            for t in range(KT):
                sp.dma_start(wtok[:, t], wtok_d[t]).then_inc(wtok_loaded[t], 16)
            sp.dma_start(win[:], win_d).then_inc(win_loaded, 16)
            sp.dma_start(wout[:], wout_d).then_inc(wout_loaded, 16)
            sp.dma_start(ws[:], ws_d).then_inc(router_loaded, 16)
            sp.dma_start(b2[:], b2_d).then_inc(router_loaded, 16)
            for e in range(NE):
                sp.dma_start(w1[0:P, e, 0], w1a_d[e]).then_inc(expert_loaded[e], 16)
                sp.dma_start(w1[0:KB + 1, e, 1], w1b_d[e]).then_inc(expert_loaded[e], 16)
                sp.dma_start(w2[:, e], w2_d[e]).then_inc(expert_loaded[e], 16)
            sp.wait_ge(u2_ready, TILES)
            sp.dma_start(rows_d.rearrange("(i p) d -> p i d", p=P), u[:]).then_inc(rows_stored, 16)
            sp.wait_ge(result_ready, TILES)
            sp.dma_start(base_d.rearrange("(i p) d -> p i d", p=P), h[:, :, 0:D + 1]).then_inc(base_stored, 16)
            sp.dma_start(out_d.rearrange("(i p) d -> p i d", p=P), h[:, :, 0:D]).then_inc(out_stored, 16)
            sp.wait_ge(overflow_known, 1)
            spare = sp.value_load(who_i[0:1, OVER:OVER + 1], min_val=0, max_val=OVER)
            for o in range(OVER):
                with sp.If(spare < OVER - o):
                    e = sp.value_load(who_i[0:1, o:o + 1], min_val=1, max_val=NR)
                    sp.wait_ge(down_ready, STEPS + o if o else TILES)
                    sp.dma_start(w1[0:P, 0, 0], w1a_d[bass.ds(e, 1)]).then_inc(overflow_loaded, 16)
                    sp.dma_start(w1[0:KB + 1, 0, 1], w1b_d[bass.ds(e, 1)]).then_inc(overflow_loaded, 16)
                    sp.dma_start(w2[:, 0], w2_d[bass.ds(e, 1)]).then_inc(overflow_loaded, 16)
            sp.wait_ge(out_stored, 16)

        @block.gpsimd
        def _(pool):
            pool.memset(ones[:], 1.0).then_inc(ones_set, 1)
            pool.memset(eps[:], EPS).then_inc(eps_set, 1)
            pool.memset(mean[:], 1.0 / QW).then_inc(mean_set, 1)
            pool.wait_ge(mean_set, 1)
            pool.memset(xr[KB:KB + 1, :, 1], 1.0).then_inc(ones_row_set, 1)
            pool.wait_ge(ones_row_set, 1)
            for t in range(1, KT):
                pool.wait_ge(squares_ready, t + 1)
                if t > 1:
                    pool.wait_ge(squares_added, t - 1)
                first = xT2[:, 0] if t == 1 else partx[:]
                pool.tensor_tensor(partx[:], first, xT2[:, t], ALU.add).then_inc(squares_added, 1)
            pool.wait_ge(vec_loaded, 16)
            pool.wait_ge(wout_loaded, 16)
            for c in range(DI // P):
                pool.tensor_scalar(wout[:, c], wout[:, c], vec[:, V_NW + c:V_NW + c + 1], None,
                                   ALU.mult).then_inc(wout_scaled, 1)
            pool.wait_ge(projected, 1)
            pool.wait_ge(wout_scaled, DI // P)
            pool.memset(M[0:SEQ, :, :, SEQ:P], 0.0).then_inc(M_blanked, 1)
            pool.wait_ge(M_blanked, 1)
            pool.memset(M[SEQ:P, :, :, 0:SEQ], 0.0).then_inc(M_blanked, 1)
            pool.wait_ge(M_blanked, 2)
            pool.wait_ge(consts_loaded, 16)
            pool.wait_ge(adt_ready, 1)
            for i in range(TILES):
                a = adt[:, i, :].unsqueeze(2).to_broadcast([P, NH, SEQ])
                c = cum.unsqueeze(1).to_broadcast([P, NH, SEQ])
                pool.tensor_tensor(segr[:, i].rearrange("p (h l) -> p h l", l=SEQ), c, a,
                                   ALU.mult).then_inc(stairs_ready, 1)

            def heads(a):
                return a.rearrange("p (h d) -> p h d", d=HD)

            def times_dt(i):
                pool.wait_ge(x_tm_ready[i // 2], i % 2 + 1)
                pool.tensor_tensor(heads(xdt[:, i]), heads(x_tm[:, i]), dt[:, i].unsqueeze(2).to_broadcast([P, NH, HD]),
                                   ALU.mult).then_inc(xdt_ready, 1)

            def times_d(i):
                pool.wait_ge(x_tm_ready[i // 2], i % 2 + 1)
                d = vec[:, V_DPAR:V_DPAR + NH].unsqueeze(2).to_broadcast([P, NH, HD])
                pool.tensor_tensor(heads(xD[:, i]), heads(x_tm[:, i]), d, ALU.mult).then_inc(xD_ready, 1)

            times_dt(0)
            for i in range(TILES):
                if i + 1 < TILES:
                    times_dt(i + 1)
                times_d(i)

            def gather(j):
                if j >= NR:
                    pool.wait_ge(rows_turned, j - NR + 1)
                pool.indirect_dma_start(xg[:, j % NR], None, rows_d,
                                        bass.IndirectOffsetOnAxis(ap=tok_u[:, j:j + 1], axis=0)
                                        ).then_inc(rows_gathered[j % NR], 16)

            def gather_base(j):
                if j >= 4:
                    pool.wait_ge(result_ready, TILES + j - 3)
                pool.indirect_dma_start(hb[:, j % 4], None, base_d,
                                        bass.IndirectOffsetOnAxis(ap=tok_u[:, j:j + 1], axis=0)
                                        ).then_inc(base_gathered[j % 4], 16)

            def scatter(j):
                pool.wait_ge(result_ready, TILES + j + 1)
                pool.indirect_dma_start(out_d, bass.IndirectOffsetOnAxis(ap=tok_w[:, j:j + 1], axis=0),
                                        y_s[:, j % 4], None, bounds_check=TOKENS - 1, oob_is_err=False
                                        ).then_inc(scattered[j % 4], 16)

            pool.wait_ge(z_ready, TILES)
            pool.wait_ge(xD_ready, TILES)
            pool.memset(uT[KB:KB + 1, 1, :], 1.0).then_inc(ones_row_set, 1)
            pool.wait_ge(ones_row_set, 2)
            pool.wait_ge(rows_stored, 16)
            pool.wait_ge(indices_ready, 1)
            for j in range(NR):
                gather(j)
            pool.wait_ge(base_stored, 16)
            for j in range(4):
                gather_base(j)
            pool.wait_ge(out_stored, 16)
            for j in range(NR):
                scatter(j)
                if j + 4 < NR:
                    gather_base(j + 4)
            pool.wait_ge(overflow_known, 1)
            spare = pool.value_load(who_i[0:1, OVER:OVER + 1], min_val=0, max_val=OVER)
            for o in range(OVER):
                with pool.If(spare < OVER - o):
                    j = NR + o
                    gather(j)
                    gather_base(j)
                    scatter(j)
                    pool.wait_ge(scattered[j % 4], 16 * (j // 4 + 1))
            for n in range(4):
                pool.wait_ge(scattered[n], 16 * (NR // 4))

        @block.scalar
        def _(act):
            done = [0]

            def link(ins):
                done[0] += 1
                ins.then_inc(act_done, 1)
                act.wait_ge(act_done, done[0])

            for g in range(KT // 2):
                act.dma_start(xT[:, 2 * g:2 * g + 2], xT_d[:, 2 * g:2 * g + 2]).then_inc(x_loaded[g], 16)
            act.dma_start(cst[:], const_d).then_inc(consts_loaded, 16)

            def fetch_table(f):
                act.activation(table_out[:], ones[:, 0:1], f)

            def root(v, **scale_bias):
                act.activation(root_t[:], v, ACT.Sqrt, **scale_bias).then_inc(root_ready, 1)

            act.wait_ge(ones_set, 1)
            fetch_table(ACT.Sqrt)
            act.wait_ge(eps_set, 1)
            act.wait_ge(vec_loaded, 16)

            def first_shift(t):
                act.wait_ge(wtok_loaded[t], 16)
                act.activation(wc[:, t, 0:D], wtok[:, t, 0], ACT.Copy,
                               scale=vec[:, V_GAMMA + t:V_GAMMA + t + 1]).then_inc(first_shift_ready, 1)

            first_shift(0)
            for t in range(KT):
                act.wait_ge(x_loaded[t // 2], 16)
                done[0] += 1
                act.activation(xT2[:, t], xT[:, t], ACT.Square).then_inc(act_done, 1)
                if t + 1 < KT:
                    first_shift(t + 1)
                act.wait_ge(act_done, done[0])
                act.activation(xT2[:, t], xT2[:, t], ACT.Copy,
                               scale=vec[:, V_MULT + t:V_MULT + t + 1]).then_inc(squares_ready, 1)
            act.wait_ge(var_ready, 1)
            root(var[:])
            act.wait_ge(sums_ready, 1)
            act.activation(csc[:, 0:D], ps[:, 6, 0:D], ACT.Copy).then_inc(csc_ready, 1)
            act.wait_ge(var_ready, 1 + TILES)
            root(bna[:, :, 1], bias=eps[:])
            act.activation(ea[:], vec[:, V_ALOG:V_ALOG + NH], ACT.Exp).then_inc(a_ready, 1)
            for half, bank in enumerate((5, 4)):
                act.wait_ge(u_turned, half + 1)
                act.activation(uT[0:DH, 0, HALF[half]], ps[0:DH, bank, HALF[0]], ACT.Copy).then_inc(uT_ready[half], 1)

            def last_tap(n):
                c = (n + 3) % NC4
                act.wait_ge(xbc_ready, n + 1)
                act.activation(acc[:, c], ps[:, c], ACT.Identity,
                               bias=vec[:, V_CB + c:V_CB + c + 1],
                               scale=vec[:, V_CW + c * TAPS + TAPS - 1:V_CW + c * TAPS + TAPS]
                               ).then_inc(last_tap_ready, 1)
            def silu_conv(n):
                c = (n + 3) % NC4
                act.wait_ge(conv_ready, n + 1)
                if c == 3:
                    act.activation(acc[0:DS, c], acc[0:DS, c], ACT.Silu).then_inc(conv_silu_ready, 1)
                    act.activation(Ct[0:DS, :], acc[DS:P, c], ACT.Silu).then_inc(conv_silu_ready, 1)
                else:
                    act.activation(acc[:, c], acc[:, c], ACT.Silu).then_inc(conv_silu_ready, 1)

            def silu_z(i):
                act.wait_ge(z_ready, i + 1)
                act.activation(zs[:, i], ps[:, 4 + i, 0:DI], ACT.Silu).then_inc(zs_ready, 1)

            last_tap(0)
            act.wait_ge(dt_projected, 1)
            act.activation(part[:, 0:P], ps[:, 4, 0:P], ACT.Copy).then_inc(dt_copied, 1)
            last_tap(1)
            act.wait_ge(dt_biased, 1)
            link(act.activation(dta[:], dtx[:], ACT.Abs))
            link(act.activation(dta[:], dta[:], ACT.Exp, scale=-1.0))
            act.activation(dta[:], dta[:], ACT.Ln, bias=1.0).then_inc(softplus_ready, 1)
            last_tap(2)
            last_tap(3)
            silu_conv(0)
            silu_conv(1)
            silu_z(0)
            silu_z(1)
            silu_conv(2)
            silu_conv(3)
            silu_z(2)
            silu_z(3)

            def decay(i):
                act.wait_ge(seg_ready, i + 1)
                act.activation(E[:, i], ps[:, 4 + i, 0:DI], ACT.Exp).then_inc(decay_ready, 1)

            decay(0)
            decay(1)
            for i in (2, 3):
                act.wait_ge(x_turned, i + 1)
                act.activation(x_tm[:, i], ps[:, XB[i], 0:DI], ACT.Copy).then_inc(x_tm_ready[1], 1)
            decay(2)
            decay(3)
            fetch_table(ACT.Sqrt)
            for i in range(TILES):
                act.wait_ge(y_gated, i + 1)
                if i:
                    act.wait_ge(y_squared, i)
                act.activation(segr[:, 0], x_tm[:, i], ACT.Square, accum_out=ss[:, i:i + 1]).then_inc(y_squared, 1)
                if i == TILES - 1:
                    act.wait_ge(y_squared, TILES)
                    root(ss[:], scale=1.0 / DI, bias=eps[:])
                act.wait_ge(y_turned, i + 1)
                act.activation(yzT[:, i], ps[:, 4 + i, 0:DI], ACT.Copy).then_inc(yT_ready, 1)
            act.wait_ge(var_ready, 1 + 2 * TILES)
            root(bna[:, :, 1], bias=eps[:])
            fetch_table(ACT.Exp)
            for half, bank in enumerate((4, 6)):
                act.wait_ge(u2_turned, half + 1)
                act.activation(uT[:, 0, HALF[half]], ps[:, bank, HALF[0]], ACT.Copy).then_inc(u2T_ready[half], 1)
            act.wait_ge(logits_less_max, 1)
            act.activation(ex[:], lg[:], ACT.Exp).then_inc(exp_ready, 1)

            def hidden(s):
                act.wait_ge(hidden_ready, s + 1)
                if s >= 2:
                    act.wait_ge(down_ready, s - 1)
                act.activation(hT[:, s % 2].rearrange("p (g f) -> p g f", g=2), ps[:, l1_banks(s), 0:FH],
                               ACT.Gelu).then_inc(gelu_ready, 1)

            for s in range(STEPS):
                hidden(s)
                if s == 1:
                    act.wait_ge(shares_turned, 1)
                    act.activation(coefT[:], ps[0:NE, 6], ACT.Copy).then_inc(coefT_ready, 1)
            spare = act.value_load(who_i[0:1, OVER:OVER + 1], min_val=0, max_val=OVER)
            for o in range(OVER):
                with act.If(spare < OVER - o):
                    hidden(STEPS + o)

        @block.vector
        def _(dve):
            done = [0]

            def link(ins):
                done[0] += 1
                ins.then_inc(dve_done, 1)
                dve.wait_ge(dve_done, done[0])

            def rsqrt(v, y):
                roots[0] += 1
                dve.wait_ge(root_ready, roots[0])
                link(dve.reciprocal(y, root_t[:]))
                link(dve.scalar_tensor_tensor(root_t[:], y, -0.5, y, ALU.mult, ALU.mult))
                link(dve.tensor_tensor(root_t[:], root_t[:], v, ALU.mult))
                link(dve.scalar_tensor_tensor(y, root_t[:], 1.5, y, ALU.add, ALU.mult))

            roots, norms = [0], [0]

            def layernorm(rows, normed):
                first = TILES * norms[0]
                norms[0] += 1

                def moments(i):
                    dve.wait_ge(h_ready, first + i + 1)
                    dve.bn_stats(bns[:, i], h[:, i, 0:D]).then_inc(bn_stats_ready, 1)

                rows(0)
                rows(1)
                rows(2)
                moments(0)
                moments(1)
                rows(3)
                moments(2)
                moments(3)
                for i in range(TILES):
                    dve.wait_ge(bn_stats_ready, first + i + 1)
                    dve.bn_aggr(bna[:, i], bns[:, i]).then_inc(var_ready, 1)
                dve.wait_ge(var_ready, 1 + first + TILES)
                link(dve.tensor_scalar(var[:], bna[:, :, 1], EPS, None, ALU.add))
                rsqrt(var[:], rstd[:])
                for i in range(TILES):
                    dve.tensor_scalar(u[:, i], h[:, i, 0:D], bna[:, i, 0:1], rstd[:, i:i + 1],
                                      ALU.subtract, ALU.mult).then_inc(normed, 1)

            dve.wait_ge(vec_loaded, 16)
            dve.tensor_copy(wc[:, :, D], vec[:, V_MULT:V_MULT + KT]).then_inc(seen_ready, 1)
            for pair in ((0,), (1,), (2,), (3,), (4, 5), (6, 7)):
                for s in range(1, SHIFTS):
                    for t in pair:
                        g = vec[:, V_GAMMA + s * KT + t:V_GAMMA + s * KT + t + 1]
                        if s == 1:
                            dve.wait_ge(first_shift_ready, t + 1)
                        else:
                            dve.wait_ge(dve_done, done[0] - (len(pair) == 2 and (t == pair[0] or s < SHIFTS - 1)))
                        ins = dve.scalar_tensor_tensor(wc[:, t, 0:D], wtok[:, t, s], g, wc[:, t, 0:D],
                                                       ALU.mult, ALU.add)
                        if s < SHIFTS - 1:
                            done[0] += 1
                            ins.then_inc(dve_done, 1)
                        else:
                            ins.then_inc(wc_ready, 1)
            dve.wait_ge(tile_sums_ready, 1)
            dve.tensor_copy(part[:], ps[:, 4, 0:2 * D]).then_inc(tile_sums_copied, 1)
            dve.wait_ge(projected, 1)
            link(dve.tensor_scalar(neg_mean[:], ps[:, 0:TILES, D], -1.0 / FEATS, None, ALU.mult))
            link(dve.tensor_tensor(square[:], neg_mean[:], neg_mean[:], ALU.mult))

            def centred(i):
                dve.scalar_tensor_tensor(h[:, i, 0:D], csc[:, 0:D], neg_mean[:, i:i + 1], ps[:, i, 0:D],
                                         ALU.mult, ALU.add).then_inc(centred_ready, 1)

            def scaled(i):
                dve.wait_ge(centred_ready, i + 1)
                dve.scalar_tensor_tensor(h[:, i, 0:D], h[:, i, 0:D], rstd[:, i:i + 1], csc[:, D:2 * D],
                                         ALU.mult, ALU.add).then_inc(h_ready, 1)

            dve.wait_ge(token_squares_ready, 1)
            link(dve.scalar_tensor_tensor(var[:], ps[:, 7, 0:TILES], 1.0 / FEATS, square[:], ALU.mult, ALU.subtract))
            dve.tensor_scalar(var[:], var[:], 0.0, EPS, ALU.max, ALU.add).then_inc(var_ready, 1)
            dve.wait_ge(csc_ready, 1)
            link(dve.tensor_tensor(csc[:, D:2 * D], ps[:, 6, D:2 * D], vec[:, V_TOKB:V_TOKB + D], ALU.add))
            for i in range(TILES):
                centred(i)
            dve.wait_ge(var_ready, 1)
            rsqrt(var[:], rstd[:])
            layernorm(scaled, u_ready)
            for half, bank in enumerate((6, 7)):
                dve.wait_ge(u_turned, half + 1)
                dve.tensor_copy(uT[0:DH, 1, HALF[half]], ps[0:DH, bank, HALF[0]]).then_inc(uT_ready[half], 1)

            def conv(n):
                c = (n + 3) % NC4
                dve.wait_ge(last_tap_ready, n + 1)
                for k in range(1, TAPS):
                    w = vec[:, V_CW + c * TAPS + TAPS - 1 - k:V_CW + c * TAPS + TAPS - k]
                    a3 = acc[:, c].rearrange("p (b l) -> p b l", l=SEQ)[:, :, k:]
                    p3 = ps[:, c].rearrange("p (b l) -> p b l", l=SEQ)[:, :, 0:SEQ - k]
                    ins = dve.scalar_tensor_tensor(a3, p3, w, a3, ALU.mult, ALU.add)
                    if k < TAPS - 1:
                        link(ins)
                    else:
                        ins.then_inc(conv_ready, 1)

            conv(0)
            dve.wait_ge(dt_turned, 1)
            dtb = vec[:, V_DTB:V_DTB + NH].unsqueeze(1).to_broadcast([P, TILES, NH])
            dt_rows = ps[:, 5, 0:P].rearrange("p (t n) -> p t n", n=QW)[:, :, 0:NH]
            dve.tensor_tensor(dtx[:], dt_rows, dtb, ALU.add).then_inc(dt_biased, 1)
            conv(1)
            dve.wait_ge(softplus_ready, 1)
            dve.wait_ge(a_ready, 1)
            link(dve.scalar_tensor_tensor(dt[:], dtx[:], 0.0, dta[:], ALU.max, ALU.add))
            eab = ea[:].unsqueeze(1).to_broadcast([P, TILES, NH])
            dve.scalar_tensor_tensor(adt[:], dt[:], -1.0, eab, ALU.mult, ALU.mult).then_inc(adt_ready, 1)
            for n in range(2, NC4):
                conv(n)
            dve.wait_ge(cb_ready, 1)
            for b in range(P // SEQ):
                r = slice(b * SEQ, (b + 1) * SEQ)
                cumb = cum[r].unsqueeze(1).to_broadcast([SEQ, TILES, SEQ])
                dve.tensor_tensor(GTm[r], ps[r, 3].rearrange("p (t l) -> p t l", l=P)[:, :, r], cumb,
                                  ALU.mult).then_inc(cb_masked, 1)
            dve.wait_ge(cb_masked, 2)

            def mix(i):
                dve.wait_ge(decay_ready, i + 1)
                dve.wait_ge(M_blanked, 2)
                for b in range(P // SEQ):
                    r = slice(b * SEQ, (b + 1) * SEQ)
                    g = GTm[r, i].unsqueeze(1).to_broadcast([SEQ, NH, SEQ])
                    dve.tensor_tensor(M[r, i, :, r], E[r, i].rearrange("p (h l) -> p h l", l=SEQ), g,
                                      ALU.mult).then_inc(M_ready, 1)

            def add_x(i):
                dve.wait_ge(y_ready, i + 1)
                dve.wait_ge(xD_ready, i + 1)
                dve.tensor_tensor(xD[:, i], ps[:, YB[i], 0:DI], xD[:, i], ALU.add).then_inc(skip_added, 1)

            def gate(i):
                dve.wait_ge(skip_added, i + 1)
                dve.wait_ge(zs_ready, TILES)
                dve.tensor_tensor(x_tm[:, i], xD[:, i], zs[:, i], ALU.mult).then_inc(y_gated, 1)

            for i in (0, 1):
                dve.wait_ge(x_turned, i + 1)
                dve.tensor_copy(x_tm[:, i], ps[:, XB[i], 0:DI]).then_inc(x_tm_ready[0], 1)
            mix(0)
            mix(1)
            mix(2)
            add_x(0)
            mix(3)
            gate(0)
            add_x(1)
            gate(1)
            add_x(2)
            gate(2)
            add_x(3)
            gate(3)
            dve.wait_ge(y_squared, TILES)
            link(dve.tensor_scalar(var[:], ss[:], 1.0 / DI, EPS, ALU.mult, ALU.add))
            rsqrt(var[:], rstd[:])

            def mixed(i):
                dve.wait_ge(out_projected, i + 1)
                dve.scalar_tensor_tensor(h[:, i, 0:D], ps[:, YB[i], 0:D], rstd[:, i:i + 1], h[:, i, 0:D],
                                         ALU.mult, ALU.add).then_inc(h_ready, 1)

            layernorm(mixed, u2_ready)
            for half, bank in enumerate((5, 7)):
                dve.wait_ge(u2_turned, half + 1)
                dve.tensor_copy(uT[0:KB, 1, HALF[half]], ps[0:KB, bank, HALF[0]]).then_inc(u2T_ready[half], 1)
            dve.wait_ge(logits_projected, 1)
            dve.tensor_copy(part[:, 0:P], ps[:, 7, 0:P]).then_inc(logits_copied, 1)
            dve.wait_ge(logits_ready, 1)
            logit_rows = ps[:, 6, 0:P].rearrange("p (t e) -> p t e", e=QW)[:, :, 0:NE]
            bsb = vec[:, V_BS:V_BS + NE].unsqueeze(1).to_broadcast([P, TILES, NE])
            iob = iota.unsqueeze(1).to_broadcast([P, TILES, NE])

            def wide(a):
                return a.unsqueeze(2).to_broadcast([P, TILES, NE])

            link(dve.tensor_tensor(lg[:], logit_rows, bsb, ALU.add))
            link(dve.tensor_reduce(m4[:], lg[:], AX.X, ALU.max))
            dve.tensor_tensor(lg[:], lg[:], wide(m4[:]), ALU.subtract).then_inc(logits_less_max, 1)
            dve.wait_ge(logits_less_max, 1)
            link(dve.tensor_scalar(oh[:], lg[:], 0.0, -float(NE), ALU.is_equal, ALU.mult))
            link(dve.tensor_tensor(oh[:], oh[:], iob, ALU.add))
            link(dve.tensor_reduce(m4[:], oh[:], AX.X, ALU.min))
            link(dve.tensor_scalar(m4[:], m4[:], float(NE), None, ALU.add))
            dve.tensor_tensor(oh[:], iob, wide(m4[:]), ALU.is_equal).then_inc(choice_ready, 1)
            dve.wait_ge(exp_ready, 1)
            link(dve.tensor_reduce(s4[:], ex[:], AX.X, ALU.add))
            link(dve.reciprocal(p4[:], s4[:]))
            link(dve.tensor_tensor(coef[:], oh[:], wide(p4[:]), ALU.mult))
            link(dve.tensor_scalar(s4[:], p4[:], -1.0, 1.0, ALU.mult, ALU.add))
            dve.tensor_tensor(coef[:, :, 0], coef[:, :, 0], s4[:], ALU.add).then_inc(shares_ready, 1)
            link(dve.tensor_tensor(gate_first[:], p4[:], oh[:, :, 0], ALU.mult))
            link(dve.tensor_tensor(h[:, :, D], p4[:], gate_first[:], ALU.subtract))
            dve.wait_ge(ranks_ready, 1)
            link(dve.tensor_copy(cnt[:], ps[:, 7, 0:2 * TILES * NR].rearrange("p (a t e) -> p a t e", a=2, e=NR)))
            link(dve.tensor_reduce(tot[:], cnt[:, 1].rearrange("p t e -> p e t"), AX.X, ALU.add))
            totb = tot[:].unsqueeze(2).to_broadcast([P, NR, OVER])
            full = iota[:, 1:OVER + 1].unsqueeze(1).to_broadcast([P, NR, OVER])
            link(dve.tensor_scalar(tot[:], tot[:], 1.0 / P, None, ALU.mult))
            link(dve.tensor_tensor(more[:], totb, full, ALU.is_gt))
            link(dve.tensor_reduce(need[:], more[:], AX.X, ALU.add))
            link(dve.tensor_tensor_scan(end[:], ones[:, 0:NR], need[:], 0.0, ALU.mult, ALU.add))
            link(dve.tensor_tensor(shift[:], end[:], need[:], ALU.subtract))
            link(dve.tensor_tensor(shift[:], shift[:], iota[:, 0:NR], ALU.subtract))
            link(dve.tensor_scalar(shift[:], shift[:], float(P), float(P * (NR - 1)), ALU.mult, ALU.add))
            for i in range(1, TILES):
                link(dve.tensor_tensor(cnt[:, 1, i], cnt[:, 1, i - 1], cnt[:, 1, i], ALU.add))
            link(dve.tensor_tensor(cnt[:, 0, 1:], cnt[:, 0, 1:], cnt[:, 1, :TILES - 1], ALU.add))
            link(dve.tensor_tensor(cnt[:, 0], cnt[:, 0], oh[:, :, 1:NE], ALU.mult))
            shiftb = shift[:].unsqueeze(1).to_broadcast([P, TILES, NR])
            link(dve.tensor_tensor(cnt[:, 1], shiftb, oh[:, :, 1:NE], ALU.mult))
            link(dve.tensor_reduce(rank[:], cnt[:], AX.X, ALU.add))
            link(dve.scalar_tensor_tensor(slot[:], rank[:, 0], float(P), rank[:, 1], ALU.is_ge, ALU.mult))
            link(dve.tensor_tensor(slot[:], slot[:], rank[:, 0], ALU.add))
            link(dve.scalar_tensor_tensor(slot[:], m4[:], float(P), slot[:], ALU.mult, ALU.add))
            link(dve.tensor_scalar(slot[:], slot[:], -float(P), 0.0, ALU.add, ALU.max))
            link(dve.tensor_copy(slot_u[:], slot[:]))
            link(dve.tensor_scalar(slot_hi[:], slot_u[:].bitcast(I32), 7, None, ALU.arith_shift_right))
            link(dve.tensor_scalar(slot_lo[:], slot_u[:].bitcast(I32), P - 1, None, ALU.bitwise_and))
            link(dve.tensor_copy(f_lo[:], slot_lo[:]))
            link(dve.scalar_tensor_tensor(f_hi[:], oh[:, :, 0], float(SLOTS + 1), slot_hi[:], ALU.mult, ALU.add))
            io_s = cst[:, C_IOTA:C_IOTA + SLOTS].unsqueeze(1).to_broadcast([P, TILES, SLOTS])
            link(dve.tensor_tensor(tile1[:], io_s, f_hi[:].unsqueeze(2).to_broadcast([P, TILES, SLOTS]), ALU.is_equal))
            for i in range(TILES):
                link(dve.tensor_scalar(tile1[:, i], tile1[:, i], cst[:, C_TOK + i:C_TOK + i + 1], None, ALU.mult))
            for i in range(TILES):
                dve.tensor_scalar(pos1[:, i], cst[:, C_LANE:C_LANE + P], f_lo[:, i:i + 1], None,
                                  ALU.is_equal).then_inc(slots_ready, 1)
            def first_result(i):
                dve.wait_ge(down_ready, i + 1)
                dve.wait_ge(biases_added, i + 1)
                dve.scalar_tensor_tensor(h[:, i, 0:D], ps[:, 4 + i % 2, 0:D], coef[:, i, 0:1], h[:, i, 0:D],
                                         ALU.mult, ALU.add).then_inc(result_ready, 1)

            def last_biases(n):
                dve.wait_ge(biases_ready, n + 1)
                for i in (2 * n, 2 * n + 1):
                    dve.tensor_tensor(h[:, i, 0:D], h[:, i, 0:D], ps[:, 6, i % 2 * 256:i % 2 * 256 + D],
                                      ALU.add).then_inc(biases_added, 1)

            last_biases(0)
            first_result(0)
            dve.wait_ge(slot_tokens_ready, 1)
            tok1 = ps[:, 7, 128:128 + SLOTS]
            link(dve.tensor_scalar(tok_f[:], tok1, 0.0, cst[:, C_TOK + TILES:C_TOK + TILES + 1],
                                   ALU.is_equal, ALU.mult))
            link(dve.tensor_scalar(tok_u[:], tok1, -1.0, 0.0, ALU.add, ALU.max))
            link(dve.scalar_tensor_tensor(tok_f[:], tok1, -1.0, tok_f[:], ALU.add, ALU.add))
            dve.tensor_copy(tok_w[:], tok_f[:]).then_inc(indices_ready, 1)
            io_n = cst[:, C_IOTA:C_IOTA + OVER].unsqueeze(2).to_broadcast([P, OVER, NR])
            link(dve.tensor_tensor(past[:], io_n, end[:].unsqueeze(1).to_broadcast([P, OVER, NR]), ALU.is_ge))
            link(dve.tensor_reduce(who[:], past[:], AX.X, ALU.add))
            link(dve.tensor_scalar(who_i[:, 0:OVER], who[:], 1.0, float(NR), ALU.add, ALU.min))
            dve.tensor_scalar(who_i[:, OVER:OVER + 1], end[:, NR - 1:NR], -1.0, float(OVER),
                              ALU.mult, ALU.add).then_inc(overflow_known, 1)
            def gathered(j):
                dve.wait_ge(rows_turned, j + 1)
                if j >= 2:
                    dve.wait_ge(hidden_ready, TILES + j - 1)
                dve.tensor_copy(xr[:, j % 2, 0], ps[:, 6 + j % 2, 0:P]).then_inc(rowsT_ready, 1)
                dve.tensor_copy(xr[0:KB, j % 2, 1], ps[0:KB, 6 + j % 2, P:2 * P]).then_inc(rowsT_ready, 1)

            def result(j):
                dve.wait_ge(down_ready, TILES + j + 1)
                if j >= 4:
                    dve.wait_ge(scattered[j % 4], 16 * (j // 4))
                b = hb[:, j % 4]
                dve.wait_ge(base_gathered[j % 4], 16 * (j // 4 + 1))
                dve.scalar_tensor_tensor(y_s[:, j % 4], ps[:, 4 + j % 2, 0:D], b[:, D:D + 1], b[:, 0:D],
                                         ALU.mult, ALU.add).then_inc(result_ready, 1)

            last_biases(1)
            first_result(1)
            first_result(2)
            gathered(0)
            gathered(1)
            first_result(3)
            for j in range(NR):
                if j + 2 < NR:
                    gathered(j + 2)
                result(j)
            spare = dve.value_load(who_i[0:1, OVER:OVER + 1], min_val=0, max_val=OVER)
            for o in range(OVER):
                with dve.If(spare < OVER - o):
                    gathered(NR + o)
                    result(NR + o)

        @block.tensor
        def _(pe):
            mm = pe.matmul
            def quad(n, total, bank, cols, lhs, rhs, opens=True):
                q = n % QUADS
                return mm(ps[q * QW:(q + 1) * QW, bank, cols], lhs.to_broadcast([P, QW]), rhs,
                          start=(opens and n < QUADS), stop=(n >= total - QUADS), skip_group_check=True,
                          tile_position=(0, q * QW))

            def beta_sums(chunks):
                for t in chunks:
                    pe.wait_ge(wtok_loaded[t], 16)
                    for s in range(SHIFTS):
                        b = vec[:, V_BETA + s * KT + t:V_BETA + s * KT + t + 1]
                        quad(t * SHIFTS + s, KT * SHIFTS, 4, slice(D, 2 * D), b, wtok[:, t, s])

            def column_sums(chunks):
                for t in chunks:
                    pe.wait_ge(wc_ready, t + 1)
                    last = quad(t, KT, 4, slice(0, D), ones[:, 0:1], wc[:, t, 0:D], opens=False)
                return last

            def project(chunks):
                for t in chunks:
                    pe.wait_ge(wc_ready, t + 1)
                    pe.wait_ge(x_loaded[t // 2], 16)
                    for i in range(TILES):
                        last = mm(ps[:, i, 0:D + 1], xT[:, t, i * P:(i + 1) * P], wc[:, t], start=(t == 0),
                                  stop=(t == KT - 1), skip_group_check=True)
                return last

            def keep_warm(n, bank):
                for _ in range(n):
                    mm(ps[:, bank], mean[:], ones[:, 0:1].to_broadcast([P, TOKENS]), start=True, stop=True)

            pe.wait_ge(ones_set, 1)
            pe.wait_ge(mean_set, 1)
            keep_warm(WARM[0], 0)
            pe.wait_ge(vec_loaded, 16)
            pe.wait_ge(seen_ready, 1)
            first, second = range(0, QUADS), range(QUADS, KT)
            for t in first:
                project((t,))
                beta_sums((t,))
            column_sums(first)
            beta_sums(second)
            project(range(QUADS, KT - 1))
            column_sums(second).then_inc(tile_sums_ready, 1)
            pe.wait_ge(squares_added, KT - 1)
            for i in range(TILES):
                last = mm(ps[:, 7, i:i + 1], partx[:, i * P:(i + 1) * P], ones[:, 0:1], start=True, stop=True)
            last.then_inc(token_squares_ready, 1)
            project(range(KT - 1, KT)).then_inc(projected, 1)
            pe.wait_ge(tile_sums_copied, 1)
            mm(ps[:, 6, 0:2 * D], mean[:], part[:], start=True, stop=True).then_inc(sums_ready, 1)
            keep_warm(WARM[1], 5)
            pe.wait_ge(bn_stats_ready, 1)
            keep_warm(WARM[2], 5)

            def turn(produced, parts, banks, turned):
                for i in range(TILES):
                    pe.wait_ge(produced, i + 1)
                    for k, cols in enumerate(parts):
                        last = pe.transpose(ps[0:cols.stop - cols.start, banks[i // 2][k], i % 2 * P:(i % 2 + 1) * P],
                                            u[:, i, cols], ident)
                    if i % 2:
                        last.then_inc(turned, 1)

            pe.wait_ge(consts_loaded, 16)
            turn(u_ready, (slice(0, DH), slice(DH, D)), ((5, 6), (4, 7)), u_turned)
            pe.wait_ge(win_loaded, 16)
            for n in range(NC4):
                c = (n + 3) % NC4
                for cols, half in ((HALF[0], 0), (HALF[1], 1)) if n == 0 else ((slice(0, TOKENS), 1),):
                    pe.wait_ge(uT_ready[half], 2)
                    for k in range(2):
                        last = mm(ps[:, c, cols], win[:, k, XC0 + c * P:XC0 + (c + 1) * P], uT[0:DH, k, cols],
                                  start=(k == 0), stop=(k == 1))
                last.then_inc(xbc_ready, 1)
                if n == 1:
                    for k in range(2):
                        for i in range(TILES):
                            last = mm(ps[i * QW:(i + 1) * QW, 4, 0:P], win[:, k, DI:DI + QW],
                                      uT[0:DH, k, i * P:(i + 1) * P], start=(k == 0), stop=(k == 1),
                                      skip_group_check=True, tile_position=(0, i * QW))
                    last.then_inc(dt_projected, 1)
                if n == 2:
                    pe.wait_ge(dt_copied, 1)
                    pe.transpose(ps[:, 5, 0:P], part[:, 0:P], ident).then_inc(dt_turned, 1)
            pe.wait_ge(dt_biased, 1)
            for i in range(TILES):
                for k in range(2):
                    last = mm(ps[:, 4 + i, 0:DI], uT[0:DH, k, i * P:(i + 1) * P], win[:, k, 0:DI],
                              start=(k == 0), stop=(k == 1))
                last.then_inc(z_ready, 1)

            def segments(i):
                pe.wait_ge(stairs_ready, i + 1)
                pe.wait_ge(zs_ready, i + 1)
                mm(ps[:, 4 + i, 0:DI], strict, segr[:, i], start=True, stop=True).then_inc(seg_ready, 1)

            def ssd(i):
                pe.wait_ge(M_ready, 2 * (i + 1))
                pe.wait_ge(xdt_ready, i + 1)
                for n in range(NH):
                    last = mm(ps[:, YB[i], n * HD:(n + 1) * HD], M[:, i, n], xdt[:, i, n * HD:(n + 1) * HD],
                              start=True, stop=True)
                last.then_inc(y_ready, 1)

            def turn_y(i):
                pe.wait_ge(y_gated, i + 1)
                for c in range(DI // P):
                    last = pe.transpose(ps[:, 4 + i, c * P:(c + 1) * P], x_tm[:, i, c * P:(c + 1) * P], ident)
                last.then_inc(y_turned, 1)

            pe.wait_ge(conv_silu_ready, 2)
            for i in range(TILES):
                r = slice(i * P, (i + 1) * P)
                last = mm(ps[:, 3, r], acc[0:DS, 3, r], Ct[0:DS, r], start=True, stop=True)
            last.then_inc(cb_ready, 1)
            segments(0)
            segments(1)
            pe.wait_ge(conv_silu_ready, NC4 + 1)
            for i in range(TILES):
                if i == 3:
                    pe.wait_ge(x_tm_ready[0], 1)
                for c in range(DI // P):
                    last = pe.transpose(ps[:, XB[i], c * P:(c + 1) * P], acc[:, c, i * P:(i + 1) * P], ident)
                last.then_inc(x_turned, 1)
            segments(2)
            segments(3)
            ssd(0)
            ssd(1)
            ssd(2)
            turn_y(0)
            ssd(3)
            turn_y(1)
            turn_y(2)

            def out_projection(i):
                pe.wait_ge(yT_ready, i + 1)
                for c in range(DI // P):
                    last = mm(ps[:, YB[i], 0:D], yzT[:, i, c * P:(c + 1) * P], wout[:, c],
                              start=(c == 0), stop=(c == DI // P - 1))
                last.then_inc(out_projected, 1)

            pe.wait_ge(wout_scaled, DI // P)
            out_projection(0)
            out_projection(1)
            turn_y(3)
            out_projection(2)
            out_projection(3)
            keep_warm(WARM[3], 6)
            turn(u2_ready, (slice(0, P), slice(P, D)), ((4, 5), (6, 7)), u2_turned)
            pe.wait_ge(u2T_ready[0], 2)
            pe.wait_ge(u2T_ready[1], 2)
            pe.wait_ge(router_loaded, 32)
            for k, rows in enumerate((slice(0, P), slice(0, KB))):
                for i in range(TILES):
                    last = mm(ps[i * QW:(i + 1) * QW, 7, 0:P], ws[rows, k], uT[rows, k, i * P:(i + 1) * P],
                              start=(k == 0), stop=(k == 1), skip_group_check=True, tile_position=(0, i * QW))
            last.then_inc(logits_projected, 1)

            def turn_rows(j):
                pe.wait_ge(rows_gathered[j % NR], 16 * (j // NR + 1))
                if j >= 2:
                    pe.wait_ge(rowsT_ready, 2 * (j - 1))
                b = 6 + j % 2
                pe.transpose(ps[:, b, 0:P], xg[:, j % NR, 0:P], ident)
                pe.transpose(ps[0:KB, b, P:2 * P], xg[:, j % NR, P:D], ident).then_inc(rows_turned, 1)

            def hidden(s):
                if s >= TILES:
                    pe.wait_ge(rowsT_ready, 2 * (s - TILES + 1))
                    xa, xb = xr[:, s % 2, 0], xr[0:KB + 1, s % 2, 1]
                else:
                    xa, xb = uT[:, 0, s * P:(s + 1) * P], uT[0:KB + 1, 1, s * P:(s + 1) * P]
                if s >= 2:
                    pe.wait_ge(gelu_ready, s - 1)
                pe.wait_ge(expert_loaded[expert(s)], 48)
                w = w1[:, expert(s)]
                for f in range(FC):
                    c = slice(f * P, (f + 1) * P)
                    o = ps[:, 2 * (s % 2) + f // 3, f % 3 * P:(f % 3 + 1) * P]
                    mm(o, w[:, 0, c], xa, start=True, stop=False)
                    last = mm(o, w[0:KB + 1, 1, c], xb, start=False, stop=True)
                last.then_inc(hidden_ready, 1)

            def down(s):
                pe.wait_ge(gelu_ready, s + 1)
                if s >= 2:
                    pe.wait_ge(result_ready, s - 1)
                for f in range(FC):
                    last = mm(ps[:, 4 + s % 2, 0:D], hT[:, s % 2, f * P:(f + 1) * P], w2[:, expert(s), f],
                              start=(f == 0), stop=(f == FC - 1))
                last.then_inc(down_ready, 1)

            pe.wait_ge(ones_row_set, 2)
            hidden(0)
            pe.wait_ge(logits_copied, 1)
            pe.transpose(ps[:, 6, 0:P], part[:, 0:P], ident).then_inc(logits_ready, 1)
            hidden(1)
            pe.wait_ge(choice_ready, 1)
            mm(ps[:, 7, 0:TILES * NR], before, oh[:, :, 1:NE], start=True, stop=True)
            mm(ps[:, 7, TILES * NR:2 * TILES * NR], ones[:], oh[:, :, 1:NE],
               start=True, stop=True).then_inc(ranks_ready, 1)
            pe.wait_ge(shares_ready, 1)
            for i in range(TILES):
                last = pe.transpose(ps[0:NE, 6, i * P:(i + 1) * P], coef[:, i], ident)
            last.then_inc(shares_turned, 1)
            down(0)

            def last_biases(n):
                for i in (2 * n, 2 * n + 1):
                    last = mm(ps[:, 6, i % 2 * 256:i % 2 * 256 + D], coefT[:, i * P:(i + 1) * P], b2[:],
                              start=True, stop=True)
                last.then_inc(biases_ready, 1)

            pe.wait_ge(coefT_ready, 1)
            last_biases(0)
            hidden(2)
            down(1)
            pe.wait_ge(slots_ready, TILES)
            for i in range(TILES):
                last = mm(ps[:, 7, 128:128 + SLOTS], pos1[:, i], tile1[:, i], start=(i == 0), stop=(i == TILES - 1))
            last.then_inc(slot_tokens_ready, 1)
            hidden(3)
            pe.wait_ge(biases_added, 2)
            last_biases(1)
            down(2)
            pe.wait_ge(biases_added, TILES)
            turn_rows(0)
            pe.wait_ge(indices_ready, 1)
            turn_rows(1)
            down(TILES - 1)
            for s in range(TILES, STEPS):
                hidden(s)
                if s + 2 < STEPS:
                    turn_rows(s + 2 - TILES)
                if s > TILES:
                    down(s - 1)
            down(STEPS - 1)
            pe.wait_ge(overflow_known, 1)
            spare = pe.value_load(who_i[0:1, OVER:OVER + 1], min_val=0, max_val=OVER)
            for o in range(OVER):
                with pe.If(spare < OVER - o):
                    turn_rows(NR + o)
                    pe.wait_ge(overflow_loaded, 48 * (o + 1))
                    hidden(STEPS + o)
                    down(STEPS + o)


def kernel(**inputs):
    import numpy as np
    import concourse.bacc as bacc
    from concourse.bass_utils import run_bass_kernel_spmd

    a = {k: np.asarray(v) for k, v in inputs.items()}

    def wrap(rows):
        full = np.zeros((KT * P,) + rows.shape[1:], rows.dtype)
        full[:rows.shape[0]] = rows
        return np.moveaxis(full.reshape((KT, P) + rows.shape[1:]), 1, 0)

    xp = np.pad(a["x"], ((0, 0), (0, 0), (1, 1), (1, 1)))
    n = a["x"].shape[2] // PATCH
    cut = np.stack([xp[:, :, PATCH * i:PATCH * i + EXT, PATCH * j:PATCH * j + EXT]
                    for i in range(n) for j in range(n)], 1)
    xT = wrap(cut.transpose(3, 2, 4, 0, 1).reshape(EXT * CH * EXT, TOKENS))

    offset = [(1, 1), (1, 0), (1, 2), (0, 1), (2, 1)]

    def spread(v):
        v = v.reshape((PATCH, PATCH, SHIFTS, CH) + v.shape[1:])
        out = np.zeros((SHIFTS, EXT, CH, EXT) + v.shape[4:], v.dtype)
        for s, (r, c) in enumerate(offset):
            out[s, r:r + PATCH, :, c:c + PATCH] = np.swapaxes(v[:, :, s], 1, 2)
        out = np.moveaxis(out, 0, 3)
        return wrap(out.reshape((EXT * CH * EXT, SHIFTS) + v.shape[4:]))

    wtok = np.ascontiguousarray(spread(a["L0_tok_W"]).swapaxes(0, 1))
    gamma = spread(a["L0_tok_gamma"]).transpose(0, 2, 1).reshape(P, SHIFTS * KT)
    beta = spread(a["L0_tok_beta"]).transpose(0, 2, 1).reshape(P, SHIFTS * KT)

    def rows(v):
        return np.broadcast_to(v.reshape(1, -1), (P, v.size))

    def cols(v):
        v = v.reshape(-1, P, v.size // v.shape[0])
        return v.transpose(1, 0, 2).reshape(P, -1)

    seen = np.zeros((EXT, CH, EXT), np.float32)
    for r, c in offset:
        seen[r:r + PATCH, :, c:c + PATCH] += 1
    vec = np.concatenate([gamma, beta, rows(a["L0_tok_b"]),
                          cols(a["L0_attn_conv_w"].reshape(-1, TAPS)), cols(a["L0_attn_conv_b"]),
                          rows(a["L0_attn_dt_bias"]), rows(a["L0_attn_A_log"]), rows(a["L0_attn_D_param"]),
                          cols(a["L0_attn_norm_w"]), rows(a["L0_ffn_bs"]), wrap(seen.reshape(-1))], 1)
    w_in = a["L0_attn_W_in"].T
    z_end, xbc_end = DI, DI + DI + 2 * DS
    win = np.concatenate([w_in[:, :z_end], w_in[:, xbc_end:], w_in[:, z_end:xbc_end]], 1)
    win = win.reshape(2, DH, -1).transpose(1, 0, 2)
    wout = a["L0_attn_W_out"].T.reshape(DI // P, P, D).transpose(1, 0, 2)
    ws = np.zeros((2, P, QW), np.float32)
    ws.reshape(2 * P, QW)[:D, :NE] = a["L0_ffn_Ws"]
    ws = ws.transpose(1, 0, 2)
    w1a = a["L0_ffn_W1"][:, 0:P]
    w1b = np.concatenate([a["L0_ffn_W1"][:, P:], a["L0_ffn_b1"][:, None]], 1)
    w2 = a["L0_ffn_W2"].reshape(NE, FC, P, D).transpose(0, 2, 1, 3)

    k, m = np.arange(P)[:, None], np.arange(P)[None, :]
    same = k // SEQ == m // SEQ
    const = np.concatenate([k == m, same & (k > m),
                            k % SEQ <= np.arange(SEQ)[None, :],
                            np.broadcast_to(np.arange(16), (P, 16)), k < m,
                            np.broadcast_to(m, (P, P)), k + 1 + P * np.arange(TILES + 1)[None, :]],
                           1).astype(np.float32)

    data = dict(xT=xT, wtok=wtok, const=const, vec=vec, win=win, wout=wout, ws=ws, b2=a["L0_ffn_b2"],
                w1a=w1a, w1b=w1b, w2=w2)
    nc = bacc.Bacc("TRN2", target_bir_lowering=False, num_devices=1)
    arrays, args = {}, []
    for name, v in data.items():
        arrays[name + "_dram"] = np.ascontiguousarray(v)
        args.append(nc.dram_tensor(name + "_dram", v.shape, mybir.dt.from_np(v.dtype), kind="ExternalInput").ap())
    args.append(nc.dram_tensor("expert_rows", (TOKENS, D), FP32, kind="Internal").ap())
    args.append(nc.dram_tensor("token_base", (TOKENS, D + 1), FP32, kind="Internal").ap())
    args.append(nc.dram_tensor("out", (TOKENS, D), FP32, kind="ExternalOutput").ap())
    vit_tower(nc, *args)
    r = run_bass_kernel_spmd(nc, [arrays], core_ids=[0])
    return r.results[0]["out"].reshape(IMGS, SEQ, D)
```
